# Optimizing a Trainium2 kernel written in Bass

```python
import numpy as np
import jax
import jax.numpy as jnp

def _softmax(x, axis=-1):
    return jax.nn.softmax(x, axis=axis)

def _gelu(x):
    return jax.nn.gelu(x, approximate=True)

def _silu(x):
    return jax.nn.silu(x)

def _sigmoid(x):
    return jax.nn.sigmoid(x)

def _layernorm(x, axis=-1, eps=1e-05):
    m = jnp.mean(x, axis=axis, keepdims=True)
    v = jnp.var(x, axis=axis, keepdims=True)
    return (x - m) / jnp.sqrt(v + eps)

def _scatter_add(tgt, idx, src, axis=0):
    return tgt.at[idx].add(src)

def _segment_sum(src, seg, n):
    return jax.ops.segment_sum(src, seg, n)
kernel_name = 'mk_recurrent_d1_jaxref_r4_b1900b'

def setup_inputs(seed: int=0):
    np.random.seed(seed)
    _w = jnp.asarray

    def _L0_attn_setup():
        import jax, jax.numpy as jnp
        import numpy as np
        from jax import lax
        B, T, D, H = (2, 1024, 256, 16)
        DK = DV = D // H
        KS = 4
        ALPHA_MIN, BETA_MAX, EPS = (0.1, 1.0, 1e-06)

        def _causal_dwconv(x, w, b):
            C, K = w.shape
            xp = jnp.pad(x, ((0, 0), (K - 1, 0), (0, 0))).transpose(0, 2, 1)
            out = lax.conv_general_dilated(xp, w[:, None, :], (1,), 'VALID', feature_group_count=C, dimension_numbers=('NCH', 'OIH', 'NCH'))
            out = out + b[None, :, None]
            return jax.nn.silu(out).transpose(0, 2, 1)

        def _l2n(t):
            return t / jnp.maximum(jnp.linalg.norm(t, axis=-1, keepdims=True), 1e-06)
        key = jax.random.key(seed)
        ks = jax.random.split(key, 20)

        def w(i, shape, sc=0.02):
            return jax.random.normal(ks[i], shape, jnp.float32) * sc
        return {'x': jax.random.normal(ks[0], (B, T, D), jnp.float32), 'Wq': w(1, (D, H * DK)), 'Wk': w(2, (D, H * DK)), 'Wv': w(3, (D, H * DV)), 'Wo': w(4, (H * DV, D)), 'Wa': w(5, (D, H)), 'ba': jnp.full((H,), 2.0, jnp.float32), 'Wb': w(6, (D, H)), 'bb': jnp.zeros((H,), jnp.float32), 'Wgd': w(7, (D, H * DV // 2)), 'Wgu': w(8, (H * DV // 2, H * DV)), 'rms_w': jnp.ones((H, DV), jnp.float32), 'qcw': w(9, (H * DK, KS), 0.1), 'qcb': jnp.zeros((H * DK,), jnp.float32), 'kcw': w(10, (H * DK, KS), 0.1), 'kcb': jnp.zeros((H * DK,), jnp.float32), 'vcw': w(11, (H * DV, KS), 0.1), 'vcb': jnp.zeros((H * DV,), jnp.float32)}
    _L0_attn_in = _L0_attn_setup()

    def _L0_ffn_setup():
        import jax, jax.numpy as jnp
        import numpy as np
        DIM = 256
        E = 8
        K = 2
        EPS = 1e-05

        def _ln(x, g, b):
            mu = jnp.mean(x, axis=-1, keepdims=True)
            var = jnp.mean(jnp.square(x - mu), axis=-1, keepdims=True)
            return (x - mu) * jax.lax.rsqrt(var + EPS) * g + b
        key = jax.random.key(seed)
        ks = jax.random.split(key, 8)
        H = 2 * DIM
        s_in = 1.0 / np.sqrt(DIM)
        s_h = 1.0 / np.sqrt(H)
        return {'x': jax.random.normal(ks[0], (2, 512, DIM), dtype=jnp.float32), 'gate_w': jax.random.uniform(ks[1], (DIM, E), minval=-s_in, maxval=s_in, dtype=jnp.float32), 'w1': jax.random.uniform(ks[2], (E, DIM, H), minval=-s_in, maxval=s_in, dtype=jnp.float32), 'b1': jax.random.uniform(ks[3], (E, H), minval=-s_in, maxval=s_in, dtype=jnp.float32), 'ln1_g': jnp.ones((E, H), dtype=jnp.float32), 'ln1_b': jnp.zeros((E, H), dtype=jnp.float32), 'w2': jax.random.uniform(ks[4], (E, H, DIM), minval=-s_h, maxval=s_h, dtype=jnp.float32), 'b2': jax.random.uniform(ks[5], (E, DIM), minval=-s_h, maxval=s_h, dtype=jnp.float32), 'ln_g': jnp.ones((DIM,), dtype=jnp.float32), 'ln_b': jnp.zeros((DIM,), dtype=jnp.float32)}
    _L0_ffn_in = _L0_ffn_setup()
    _d = {'L0_attn_x': _L0_attn_in['x'], 'L0_attn_Wq': _L0_attn_in['Wq'], 'L0_attn_Wk': _L0_attn_in['Wk'], 'L0_attn_Wv': _L0_attn_in['Wv'], 'L0_attn_Wo': _L0_attn_in['Wo'], 'L0_attn_Wa': _L0_attn_in['Wa'], 'L0_attn_ba': _L0_attn_in['ba'], 'L0_attn_Wb': _L0_attn_in['Wb'], 'L0_attn_bb': _L0_attn_in['bb'], 'L0_attn_Wgd': _L0_attn_in['Wgd'], 'L0_attn_Wgu': _L0_attn_in['Wgu'], 'L0_attn_rms_w': _L0_attn_in['rms_w'], 'L0_attn_qcw': _L0_attn_in['qcw'], 'L0_attn_qcb': _L0_attn_in['qcb'], 'L0_attn_kcw': _L0_attn_in['kcw'], 'L0_attn_kcb': _L0_attn_in['kcb'], 'L0_attn_vcw': _L0_attn_in['vcw'], 'L0_attn_vcb': _L0_attn_in['vcb'], 'L0_ffn_gate_w': _L0_ffn_in['gate_w'], 'L0_ffn_w1': _L0_ffn_in['w1'], 'L0_ffn_b1': _L0_ffn_in['b1'], 'L0_ffn_ln1_g': _L0_ffn_in['ln1_g'], 'L0_ffn_ln1_b': _L0_ffn_in['ln1_b'], 'L0_ffn_w2': _L0_ffn_in['w2'], 'L0_ffn_b2': _L0_ffn_in['b2'], 'L0_ffn_ln_g': _L0_ffn_in['ln_g'], 'L0_ffn_ln_b': _L0_ffn_in['ln_b']}
    _x0 = _d['L0_attn_x']
    _d['L0_attn_x'] = jax.random.normal(jax.random.fold_in(jax.random.key(seed), 1), (8, 1024, 256), dtype=_x0.dtype)
    del _x0
    return _d

def reference(L0_attn_x, L0_attn_Wq, L0_attn_Wk, L0_attn_Wv, L0_attn_Wo, L0_attn_Wa, L0_attn_ba, L0_attn_Wb, L0_attn_bb, L0_attn_Wgd, L0_attn_Wgu, L0_attn_rms_w, L0_attn_qcw, L0_attn_qcb, L0_attn_kcw, L0_attn_kcb, L0_attn_vcw, L0_attn_vcb, L0_ffn_gate_w, L0_ffn_w1, L0_ffn_b1, L0_ffn_ln1_g, L0_ffn_ln1_b, L0_ffn_w2, L0_ffn_b2, L0_ffn_ln_g, L0_ffn_ln_b):

    def _L0_attn_ref(x, Wq, Wk, Wv, Wo, Wa, ba, Wb, bb, Wgd, Wgu, rms_w, qcw, qcb, kcw, kcb, vcw, vcb):
        import jax, jax.numpy as jnp
        import numpy as np
        from jax import lax
        B, T, D, H = (2, 1024, 256, 16)
        DK = DV = D // H
        KS = 4
        ALPHA_MIN, BETA_MAX, EPS = (0.1, 1.0, 1e-06)

        def _causal_dwconv(x, w, b):
            C, K = w.shape
            xp = jnp.pad(x, ((0, 0), (K - 1, 0), (0, 0))).transpose(0, 2, 1)
            out = lax.conv_general_dilated(xp, w[:, None, :], (1,), 'VALID', feature_group_count=C, dimension_numbers=('NCH', 'OIH', 'NCH'))
            out = out + b[None, :, None]
            return jax.nn.silu(out).transpose(0, 2, 1)

        def _l2n(t):
            return t / jnp.maximum(jnp.linalg.norm(t, axis=-1, keepdims=True), 1e-06)
        Bx, Tx, _ = x.shape
        BH = Bx * H
        q = _causal_dwconv(x @ Wq, qcw, qcb)
        k = _causal_dwconv(x @ Wk, kcw, kcb)
        v = _causal_dwconv(x @ Wv, vcw, vcb)

        def heads(t, d):
            return t.reshape(Bx, Tx, H, d).transpose(0, 2, 1, 3).reshape(BH, Tx, d)
        Q = _l2n(heads(q, DK))
        Kh = _l2n(heads(k, DK))
        V = heads(v, DV)
        alpha = jnp.clip(jax.nn.sigmoid(x @ Wa + ba), ALPHA_MIN, 1.0)
        beta = jnp.minimum(jax.nn.sigmoid(x @ Wb + bb), BETA_MAX)
        alpha = alpha.transpose(0, 2, 1).reshape(BH, Tx)
        beta = beta.transpose(0, 2, 1).reshape(BH, Tx)

        def step(S, inp):
            qt, kt, vt, at, bt = inp
            v_hat = jnp.einsum('bij,bi->bj', S, kt)
            err = vt - v_hat
            S = at[:, None, None] * S + bt[:, None, None] * (kt[:, :, None] * err[:, None, :])
            o = jnp.einsum('bij,bi->bj', S, qt)
            return (S, o)
        S0 = jnp.zeros((BH, DK, DV), x.dtype)
        _, O = lax.scan(step, S0, (Q.swapaxes(0, 1), Kh.swapaxes(0, 1), V.swapaxes(0, 1), alpha.T, beta.T))
        O = O.transpose(1, 0, 2).reshape(Bx, H, Tx, DV)
        O = O * lax.rsqrt(jnp.mean(O * O, -1, keepdims=True) + EPS) * rms_w[None, :, None, :]
        g = jax.nn.sigmoid(jax.nn.silu(x @ Wgd) @ Wgu).reshape(Bx, Tx, H, DV).transpose(0, 2, 1, 3)
        O = (O * g).transpose(0, 2, 1, 3).reshape(Bx, Tx, H * DV)
        return O @ Wo

    def _L0_ffn_ref(x, gate_w, w1, b1, ln1_g, ln1_b, w2, b2, ln_g, ln_b):
        import jax, jax.numpy as jnp
        import numpy as np
        DIM = 256
        E = 8
        K = 2
        EPS = 1e-05

        def _ln(x, g, b):
            mu = jnp.mean(x, axis=-1, keepdims=True)
            var = jnp.mean(jnp.square(x - mu), axis=-1, keepdims=True)
            return (x - mu) * jax.lax.rsqrt(var + EPS) * g + b
        shape = x.shape
        xf = x.reshape(-1, shape[-1])
        gates = jax.nn.softmax(xf @ gate_w, axis=-1)
        topw, topi = jax.lax.top_k(gates, K)
        topw = topw / jnp.sum(topw, axis=-1, keepdims=True)
        combine = jnp.sum(topw[:, :, None] * jax.nn.one_hot(topi, E, dtype=xf.dtype), axis=1)
        h = jnp.einsum('td,edh->teh', xf, w1) + b1
        h = _ln(h, ln1_g, ln1_b)
        h = jax.nn.gelu(h, approximate=False)
        y = jnp.einsum('teh,ehd->ted', h, w2) + b2
        out = jnp.einsum('ted,te->td', y, combine)
        out = _ln(out + xf, ln_g, ln_b)
        return out.reshape(shape)
    x = L0_attn_x
    xn = _layernorm(x, axis=-1)
    s = _L0_attn_ref(xn, L0_attn_Wq, L0_attn_Wk, L0_attn_Wv, L0_attn_Wo, L0_attn_Wa, L0_attn_ba, L0_attn_Wb, L0_attn_bb, L0_attn_Wgd, L0_attn_Wgu, L0_attn_rms_w, L0_attn_qcw, L0_attn_qcb, L0_attn_kcw, L0_attn_kcb, L0_attn_vcw, L0_attn_vcb)
    g = _silu(_L0_ffn_ref(xn, L0_ffn_gate_w, L0_ffn_w1, L0_ffn_b1, L0_ffn_ln1_g, L0_ffn_ln1_b, L0_ffn_w2, L0_ffn_b2, L0_ffn_ln_g, L0_ffn_ln_b))
    x = x + s * g
    return x

_drawn_inputs = setup_inputs


def setup_inputs(seed=0):
    import zlib

    import numpy as np

    out = dict(_drawn_inputs(seed))
    spreads = {'L0_attn_ba': (2.0, 0.6),
     'L0_attn_bb': (0.0, 0.8),
     'L0_attn_rms_w': (1.0, 0.6),
     'L0_attn_qcb': (0.0, 0.1),
     'L0_attn_kcb': (0.0, 0.1),
     'L0_attn_vcb': (0.0, 0.1),
     'L0_ffn_ln1_g': (1.0, 0.6),
     'L0_ffn_ln1_b': (0.0, 0.8),
     'L0_ffn_ln_g': (1.0, 0.6),
     'L0_ffn_ln_b': (0.0, 0.8)}
    factors = {'L0_attn_Wa': 8.0,
     'L0_attn_Wb': 5.88,
     'L0_attn_Wgd': 8.0,
     'L0_attn_Wgu': 8.0,
     'L0_ffn_b1': 8.0,
     'L0_ffn_b2': 8.0}
    for name, (base, spread) in spreads.items():
        noise = np.random.default_rng([zlib.crc32(name.encode()), seed]).standard_normal(out[name].shape)
        drawn = base * np.exp(spread * noise) if base else spread * noise
        out[name] = jnp.asarray(drawn.astype(out[name].dtype))
    for name, factor in factors.items():
        out[name] = (out[name] * factor).astype(out[name].dtype)
    return out
```

```python
from contextlib import ExitStack

import concourse.bass as bass
from concourse import mybir

F32 = mybir.dt.float32
F16 = mybir.dt.float16
I32 = mybir.dt.int32
ALU = mybir.AluOpType
ACT = mybir.ActivationFunctionType
AX = mybir.AxisListType.X

P = 128
B, T, D = 8, 1024, 256
H, DH = 16, 16
E, HID = 8, 512
TB = 128
NB = T // TB
KC = D // P
MC = HID // P
TAPS = 4
HALO = TAPS - 1
GRP = 3 * KC
HB = B // 2
HT = HB * TB
SUB = HT // P
UNITS = 2 * E
GT = 8
NG = TB // GT
STEP = 9
LN_EPS = 1e-5
RMS_EPS = 1e-6
NORM_MIN = 1e-12
HEAD_STEPS = 3 * 5 + 2 + 3 + 2 * (1 + 3 * 4) + 5
GATE_STEPS = 10
GROUP_STEPS = GT * STEP + 5
BLOCK_STEPS = 2 + 3 * 3
MAGIC = float(0x5F3759DF)


def bass_delta_moe(nc, x, wqkv, cw, wab, wgd, wgu, wo, gate, w1, w2, b2, rows, cols, out):
    ctx = ExitStack()
    with ctx:
        def sb(name, shape, dt=F32):
            return ctx.enter_context(nc.sbuf_tensor(name, shape, dt))

        def ps(name, shape):
            return ctx.enter_context(nc.psum_tensor(name, shape, F32))

        def sem(name):
            return ctx.enter_context(nc.semaphore(name))

        qkv_dram = nc.dram_tensor("qkv_scratch", (2, 3, B, H * DH, TB), F32, kind="Internal").ap()
        ab_dram = nc.dram_tensor("ab_scratch", (2, 2, B, H, TB), F32, kind="Internal").ap()
        o_dram = nc.dram_tensor("o_scratch", (2, B, H * DH, TB), F32, kind="Internal").ap()
        ecol_dram = nc.dram_tensor("ecol_scratch", (E, P, 3 * MC), F32, kind="Internal").ap()
        w1_dram = nc.dram_tensor("w1_scratch", (E, P, 2 * KC * HID), F16, kind="Internal").ap()

        ident = sb("ident", [P, P])
        over_hid = sb("over_hid", [P, P])
        below = sb("below", [P, E, E])
        minus_half = sb("minus_half", [P, P])
        CONSTS = (1.5, -1.0)
        consts = sb("consts", [P, len(CONSTS)])
        wp_hi = sb("wp_hi", [P, KC, TAPS, 3 * D], F16)
        wp_lo = sb("wp_lo", [P, KC, TAPS, 3 * D], F16)
        wab_hi = sb("wab_hi", [P, KC, 2 * H], F16)
        wab_lo = sb("wab_lo", [P, KC, 2 * H], F16)
        wgd_hi = sb("wgd_hi", [P, KC, P], F16)
        wgd_lo = sb("wgd_lo", [P, KC, P], F16)
        wgu_sb = sb("wgu_sb", [P, D])
        wo_sb = sb("wo_sb", [P, KC, D])
        gate_sb = sb("gate_sb", [P, KC, E])
        b2_sb = sb("b2_sb", [P, D])
        rows_sb = sb("rows_sb", [P, 2, D])
        NCOL = cols.shape[1]
        cols_sb = sb("cols_sb", [P, NCOL])
        conv_b = cols_sb[:, 0:GRP]
        ab_b = cols_sb[0:2 * H, GRP:GRP + 1]
        rms_col = cols_sb[:, GRP + 1:GRP + 1 + KC]
        ECOL = 3 * MC
        expert_cols = cols_sb[:, GRP + 3:GRP + 3 + E * ECOL].rearrange("p (e n m) -> p e n m", e=E, n=3)
        b1_col = expert_cols[:, :, 2, :]
        b1_mean = sb("b1_mean", [P, E])
        w_mean = sb("w_mean", [P, E * KC])

        x_in = sb("x_in", [P, 2, D])
        junk = sb("junk", [P, D])
        stat = sb("stat", [P, 2, 6])
        acc = sb("acc", [P, 2, B, D])
        xT32 = sb("xT32", [P, 2, KC, P])
        xT_hi = sb("xT_hi", [P, 2, KC, B, HALO + TB], F16)
        xT_lo = sb("xT_lo", [P, 2, KC, B, HALO + TB], F16)
        logits = sb("logits", [P, B, E])
        lmax = sb("lmax", [P, B])
        shifted = sb("shifted", [P, B, E])
        expd = sb("expd", [P, B, E])
        rank = sb("rank", [P, B, E])
        csum = sb("csum", [P, B])
        comb = sb("comb", [P, 2, B, 32])
        combT = sb("combT", [P, 2, P])

        kq = sb("kq", [P, 2, 2, DH, TB])
        bv = sb("bv", [P, 2, DH, TB])
        decay = sb("decay", [P, 2, TB])
        beta = sb("beta", [P, TB])
        c_v = sb("c_v", [P, 2, TB])
        c_q = sb("c_q", [P, 2, TB])
        c_qk = sb("c_qk", [P, 2, TB])
        head_tmp = sb("head_tmp", [P, DH, TB])
        head_norm = sb("head_norm", [P, 2, TB])
        head_sq = sb("head_sq", [P, TB])
        r_k = sb("r_k", [P, TB])
        r_q = sb("r_q", [P, TB])
        state = sb("state", [P, 2, DH, DH])
        prod_k = sb("prod_k", [P, DH, DH])
        prod_q = sb("prod_q", [P, DH, DH])
        outer = sb("outer", [P, DH, DH])
        cmp_gt = prod_k[:, :, :].rearrange("p a b -> p (a b)").bitcast(F16).rearrange("p (b e f) -> p b e f", b=B, e=E)
        cmp_eq = outer[:, :, :].rearrange("p a b -> p (a b)").bitcast(F16).rearrange("p (b e f) -> p b e f", b=B, e=E)
        ks = sb("ks", [P, DH])
        qs = sb("qs", [P, GT, DH])
        upd = sb("upd", [P, GT, DH])
        o_t1 = sb("o_t1", [P, GT, DH])
        o_t2 = sb("o_t2", [P, GT, DH])
        o_sq = sb("o_sq", [P, GT, DH])
        o_all = sb("o_all", [P, DH, TB])
        o_ms = sb("o_ms", [P, TB])
        o_r = sb("o_r", [P, TB])
        o_n = sb("o_n", [P, TB])

        w1_sb = sb("w1_sb", [P, 2, 2, KC, HID], F16)
        w2_sb = sb("w2_sb", [P, 2, MC, D])
        ecol_sb = sb("ecol_sb", [P, 2, 3, MC])
        share = sb("share", [P, 4, HB])
        hid = sb("hid", [P, 2, MC, HT])
        sq = sb("sq", [P, MC, HT])
        var_sb = sb("var_sb", [P, SUB])
        rstd = sb("rstd", [P, SUB])
        rstd_b = sb("rstd_b", [P, HT])
        y_sb = sb("y_sb", [P, SUB, D])

        oT = head_tmp
        oT_v = oT[:, :, :].rearrange("p (g b) t -> p g b t", g=KC)
        s_sb = sb("s_sb", [P, D])
        x_res = sb("x_res", [P, 2, D])
        fstat = sb("fstat", [P, 6])
        sq_flat = sq[:, :, :].rearrange("p m t -> p (m t)")
        gate_o = sq[:, 0:KC, :]
        gd_sb = sq[:, KC, :]
        z = sq_flat[:, 3 * HT:3 * HT + D]
        z2 = sq_flat[:, 3 * HT + D:3 * HT + 2 * D]
        stage = y_sb[:, :, :].rearrange("p c d -> p (c d)").rearrange("p (s t) -> p s t", s=2)
        ab_stage = hid[0:2 * H, 0, 0:2, :]
        res = sb("res", [P, 2, D])
        pool_spare = sb("pool_spare", [P, 1])

        h_ps = ps("h_ps", [P, MC, HT])
        y_ps = ps("y_ps", [P, SUB, D])
        r_ps = ps("r_ps", [P, HT])
        m_ps = ps("m_ps", [P, HT])


        names = """w_in w1_raw0 w1_raw1 w1_free w1_split w1_out const_ready wsplit setup_done
        b1_ps b1_ready dsetup
        x_in0 x_in1 xctr xsum xsq xneg xstat xpow xn_ready x_lo halo_done m_full m_free
        qkv_out0 qkv_out1 ab_out heads_in head_step heads_ready guess gmax gexp comb_ready dgate
        step block_step o_ready o_out
        w_e0 w_e1 h_done sq_done sq_part sq_sum v_ps v_sb v_rstd rb_ps rb_sb t_done a_done
        b2_part y_full y_free y_added
        oT_in og_done fsum fsum2 fneg fctr frstd z_norm fsq fstep z_ready z_silu res_done x_res0 x_res1 out0 out1""".split()
        s = {n: sem(n) for n in names}
        x_in_s = (s["x_in0"], s["x_in1"])
        qkv_out_s = (s["qkv_out0"], s["qkv_out1"])
        w_e_s = (s["w_e0"], s["w_e1"])
        x_res_s = (s["x_res0"], s["x_res1"])
        out_s = (s["out0"], s["out1"])
        w1_raw_s = (s["w1_raw0"], s["w1_raw1"])
        HAND = 2
        FIRST = 1
        N_CONST = 8 + len(CONSTS)
        N_IN = 13

        M_PREP, M_EXP, M_FIN = 2 * B + 2 * GRP + 2, 2, 2 * (3 + HB)

        def m_prep(tau):
            return 0 if isinstance(tau, int) and tau == 0 else tau * (M_PREP + M_EXP) + (tau - 1) * M_FIN

        def m_exp(tau):
            return (tau + 1) * M_PREP + tau * (M_EXP + M_FIN)

        def m_fin(tau):
            n_prep = NB if isinstance(tau, int) and tau == NB - 1 else tau + 2
            n_exp = NB if isinstance(tau, int) and tau == NB - 1 else tau + 2
            return n_prep * M_PREP + (tau + 1) * M_EXP + tau * M_FIN

        Y = 2 + UNITS

        taps_b = hid[:, :, :, :].rearrange("p a m t -> p (a m t)")[:, 0:TAPS * 3 * D].rearrange(
            "p (k c) -> p k c", k=TAPS)
        wqkv_raw = sq[:, :, :].rearrange("p m t -> p (m t)")[:, 0:KC * 3 * D].rearrange("p (k c) -> p k c", k=KC)
        wtap = o_all[:, :, :].rearrange("p a b -> p (a b)")[:, 0:3 * D]
        small_raw = x_res[:, :, :].rearrange("p s d -> p (s d)")
        wgd_raw = small_raw[:, 0:KC * P].rearrange("p (k c) -> p k c", k=KC)
        wab_raw = small_raw[:, KC * P:KC * P + KC * 2 * H].rearrange("p (k c) -> p k c", k=KC)
        w1_raw = y_sb[:, :, :].rearrange("p a b -> p (a b)").rearrange("p (s h) -> p s h", s=2)
        w1_ctr = res[:, :, :].rearrange("p s d -> p (s d)")
        w1_parts = w1_sb[:, 0, :, :, :]

        block = ctx.enter_context(nc.Block())

        def schedule(eng, prep, experts, final):
            prep(0, 0)
            experts(0, 0)
            prep(1, 1)
            with eng.Fori(0, (NB - 2) // 2) as m:
                for j in range(2):
                    tau = m * 2 + (j + 1)
                    final(tau - 1, j % 2)
                    experts(tau, (j + 1) % 2)
                    prep(tau + 1, j % 2)
            final(NB - 2, 0)
            experts(NB - 1, 1)
            final(NB - 1, 1)

        def pipelined(eng, first, turn, following, last):
            first()
            with eng.Fori(0, E // 2 - 1) as ep:
                for j in range(4):
                    turn(ep, j)
                    following(ep, j + 1)
                    last(ep, j)
            for j in range(4):
                turn(E // 2 - 1, j)
                if j < 3:
                    following(E // 2 - 1, j + 1)
                last(E // 2 - 1, j)

        def tile_of(dram, tau, b):
            return dram[bass.ds(b, 1), bass.ds(tau * TB, TB), :].rearrange("o t d -> (o t) d")

        @block.sync
        def _(sp):
            for t_ in ("xn_ready", "res_done"):
                sp.sem_inc(s[t_], HAND)
            for t_ in ("y_full", "rb_sb", "step"):
                sp.sem_inc(s[t_], FIRST)
            sp.sem_inc(s["o_out"], 16 * FIRST)
            sp.dma_start(cols_sb[:, :], cols).then_inc(s["w_in"], 16)
            sp.dma_start(rows_sb[:, :, :], rows.rearrange("(o r) d -> o r d", o=1).broadcast_to([P, 2, D])).then_inc(s["w_in"], 16)
            sp.dma_start(taps_b, cw.rearrange("(o k) c -> o k c", o=1).broadcast_to([P, TAPS, 3 * D])).then_inc(s["w_in"], 16)
            sp.dma_start(wqkv_raw, wqkv.rearrange("(k p) c -> p k c", p=P)).then_inc(s["w_in"], 16)
            sp.dma_start(wgd_raw, wgd.rearrange("(k p) c -> p k c", p=P)).then_inc(s["w_in"], 16)
            sp.dma_start(wab_raw, wab.rearrange("(k p) c -> p k c", p=P)).then_inc(s["w_in"], 16)
            sp.dma_start(wgu_sb[:, :], wgu).then_inc(s["w_in"], 16)
            sp.dma_start(wo_sb[:, :, :], wo.rearrange("(k p) c -> p k c", p=P)).then_inc(s["w_in"], 16)
            sp.dma_start(gate_sb[:, :, :], gate.rearrange("(k p) c -> p k c", p=P)).then_inc(s["w_in"], 16)
            for q in range(4):
                sp.dma_start(b2_sb[32 * q:32 * q + E, :], b2).then_inc(s["w_in"], 16)
            for e in range(E):
                for k in range(KC):
                    if e > 0:
                        sp.wait_ge(s["w1_free"], (e - 1) * KC + k + 1)
                    sp.dma_start(w1_raw[:, k, :], w1[e, k * P:(k + 1) * P, :]).then_inc(w1_raw_s[k], 16)
                sp.wait_ge(s["w1_split"], e + 1)
                sp.dma_start(w1_dram[e], w1_parts.rearrange("p h k c -> p (h k c)")).then_inc(s["w1_out"], 16)
            sp.wait_ge(s["b1_ready"], 1)
            sp.dma_start(ecol_dram.rearrange("e p c -> p e c"),
                         expert_cols.rearrange("p e n m -> p e (n m)")).then_inc(s["w1_out"], 16)
            sp.wait_ge(s["w1_out"], 16 * (E + 1))

            def prep(tau, par):
                with sp.Fori(0, B // 2) as bp:
                    for slot in range(2):
                        b = bp * 2 + slot
                        sp.wait_ge(s["xn_ready"], tau * B + b + 1)
                        sp.dma_start(x_in[:, slot, :], tile_of(x, tau, b)).then_inc(x_in_s[slot], 16)
                for g in range(GRP):
                    for half in range(2):
                        sp.wait_ge(s["m_free"], m_prep(tau) + 2 * B + g * 2 + half + 1)
                        dst = qkv_dram[par, g // KC, half * HB:(half + 1) * HB, (g % KC) * P:(g % KC + 1) * P, :]
                        sp.dma_start(dst.rearrange("b c t -> c b t"),
                                     stage[:, half, :].rearrange("p (b t) -> p b t", b=HB)).then_inc(qkv_out_s[half], 16)
                for half in range(2):
                    sp.wait_ge(s["m_free"], m_prep(tau) + 2 * B + 2 * GRP + half + 1)
                    for which in range(2):
                        dst = ab_dram[par, which, half * HB:(half + 1) * HB, :, :]
                        sp.dma_start(dst.rearrange("b h t -> h b t"),
                                     ab_stage[which * H:(which + 1) * H, half, :].rearrange("p (b t) -> p b t", b=HB)).then_inc(s["ab_out"], 16)
                for half in range(2):
                    sp.wait_ge(qkv_out_s[half], (tau + 1) * GRP * 16)
                sp.wait_ge(s["ab_out"], (tau + 1) * 4 * 16)
                if not (isinstance(tau, int) and tau < 2):
                    sp.wait_ge(s["o_ready"], tau - 1)
                if not (isinstance(tau, int) and tau < 1):
                    sp.wait_ge(s["heads_ready"], tau)
                for src, dst in ((1, kq[:, par, 0, :, :]), (0, kq[:, par, 1, :, :]), (2, bv[:, par, :, :])):
                    sp.dma_start(dst.rearrange("p d t -> p (d t)"),
                                 qkv_dram[par, src].rearrange("b (h d) t -> (b h) (d t)", h=H)).then_inc(s["heads_in"], 16)
                for which, dst in ((0, decay[:, par, :]), (1, beta[:, :])):
                    sp.dma_start(dst, ab_dram[par, which].rearrange("b h t -> (b h) t")).then_inc(s["heads_in"], 16)

            def experts(tau, par):
                with sp.Fori(0, E // 2) as ep:
                    for slot in range(2):
                        e = ep * 2 + slot
                        sp.wait_ge(s["y_full"], FIRST + tau * Y + ep * 4 + slot * 2)
                        sp.dma_start(w1_sb[:, slot, :, :, :].rearrange("p h k c -> p (h k c)"),
                                     w1_dram[bass.ds(e, 1)].rearrange("o p c -> (o p) c")).then_inc(w_e_s[slot], 16)
                        sp.dma_start(w2_sb[:, slot, :, :],
                                     w2[bass.ds(e, 1)].rearrange("o (m p) d -> p (o m) d", p=P)).then_inc(w_e_s[slot], 16)
                        sp.dma_start(ecol_sb[:, slot, :, :].rearrange("p n m -> p (n m)"),
                                     ecol_dram[bass.ds(e, 1)].rearrange("o p c -> (o p) c")).then_inc(w_e_s[slot], 16)

            def final(tau, par):
                blocks_in = NB if isinstance(tau, int) and tau == NB - 1 else tau + 2
                sp.wait_ge(s["o_ready"], tau + 1)
                sp.dma_start(o_dram[par].rearrange("b (h j) t -> (b h) (j t)", h=H),
                             o_all[:, :, :].rearrange("p j t -> p (j t)")).then_inc(s["o_out"], 16)
                sp.wait_ge(s["o_out"], 16 * FIRST + (tau + 1) * 16)
                sp.wait_ge(s["head_step"], blocks_in * HEAD_STEPS - (HEAD_STEPS - 3 * 5 - 2))
                for g in range(KC):
                    sp.dma_start(oT_v[:, g, :, :],
                                 o_dram[par].rearrange("b (g c) t -> g c b t", g=KC)[g]).then_inc(s["oT_in"], 16)
                with sp.Fori(0, B // 2) as bp:
                    for slot in range(2):
                        b = bp * 2 + slot
                        sp.wait_ge(s["res_done"], tau * B + b + 1)
                        sp.dma_start(x_res[:, slot, :], tile_of(x, tau, b)).then_inc(x_res_s[slot], 16)
                    for slot in range(2):
                        b = bp * 2 + slot
                        sp.wait_ge(s["res_done"], tau * B + b + HAND + 1)
                        sp.dma_start(tile_of(out, tau, b), res[:, slot, :]).then_inc(out_s[slot], 16)

            schedule(sp, prep, experts, final)
            for q in range(2):
                sp.wait_ge(out_s[q], NB * (B // 2) * 16)

        @block.tensor
        def _(pe):
            def split3(out_, w_hi, w_lo, x_hi, x_lo, n, of):
                parts = ((w_hi, x_hi), (w_hi, x_lo), (w_lo, x_hi))
                for i, (a_, b_) in enumerate(parts):
                    last = nc.tensor.matmul(out_, a_, b_, start=(n == 0 and i == 0), stop=(n == of - 1 and i == 2))
                return last

            pe.wait_ge(s["const_ready"], N_CONST)
            pe.wait_ge(s["w_in"], N_IN * 16)
            nc.tensor.matmul(r_ps[:, 0:E * MC].rearrange("p (e m) -> p e m", m=MC), over_hid[:, :], b1_col, start=True, stop=True).then_inc(s["b1_ps"], 1)
            pe.wait_ge(s["setup_done"], 1)
            pe.wait_ge(s["b1_ready"], 1)

            def prep(tau, par):
                for bp in range(B // 2):
                    for slot in range(2):
                        i = m_prep(tau) + bp * 4 + slot * 2
                        pe.wait_ge(s["xn_ready"], tau * B + bp * 2 + slot + HAND + 1)
                        pe.wait_ge(s["m_free"], i)
                        for k in range(KC):
                            last = nc.tensor.transpose(m_ps[:, k * P:(k + 1) * P],
                                                       acc[:, par, bp * 2 + slot, k * P:(k + 1) * P],
                                                       ident[:, :])
                        last.then_inc(s["m_full"], 1)
                        pe.wait_ge(s["m_free"], i + 1)
                        for k in range(KC):
                            last = nc.tensor.matmul(m_ps[:, 0:E], xT32[:, slot, k, :], gate_sb[:, k, :],
                                                    start=k == 0, stop=k == KC - 1)
                        last.then_inc(s["m_full"], 1)
                pe.wait_ge(s["x_lo"], (tau + 1) * B)
                pe.wait_ge(s["halo_done"], (tau + 1) * 2)
                for g in range(GRP):
                    for half in range(2):
                        pe.wait_ge(s["m_free"], m_prep(tau) + 2 * B + g * 2 + half)
                        o_ = m_ps[:, :].rearrange("p (b t) -> p b t", b=HB)
                        for n in range(KC * TAPS):
                            k, tap = n // TAPS, n % TAPS
                            rows_ = slice(half * HB, (half + 1) * HB)
                            last = split3(o_, wp_hi[:, k, tap, g * P:(g + 1) * P], wp_lo[:, k, tap, g * P:(g + 1) * P],
                                          xT_hi[:, par, k, rows_, tap:tap + TB], xT_lo[:, par, k, rows_, tap:tap + TB],
                                          n, KC * TAPS)
                        last.then_inc(s["m_full"], 1)
                for half in range(2):
                    pe.wait_ge(s["m_free"], m_prep(tau) + 2 * B + 2 * GRP + half)
                    o_ = m_ps[0:2 * H, :].rearrange("p (b t) -> p b t", b=HB)
                    for k in range(KC):
                        rows_ = slice(half * HB, (half + 1) * HB)
                        last = split3(o_, wab_hi[:, k, :], wab_lo[:, k, :], xT_hi[:, par, k, rows_, HALO:],
                                      xT_lo[:, par, k, rows_, HALO:], k, KC)
                    last.then_inc(s["m_full"], 1)

            def experts(tau, par):
                pe.wait_ge(s["comb_ready"], tau + 1)
                for q in range(2):
                    i = m_exp(tau) + q
                    pe.wait_ge(s["m_free"], i)
                    nc.tensor.transpose(m_ps[:, 0:P], comb[:, par, q * HB:(q + 1) * HB, :].rearrange("p b c -> p (b c)"),
                                        ident[:, :]).then_inc(s["m_full"], 1)
                    pe.wait_ge(s["m_free"], i + 1)
                    pe.wait_ge(s["y_free"], tau * Y + q)
                    for b in range(HB):
                        if b > 0:
                            pe.wait_ge(s["b2_part"], (tau * 2 + q) * (HB - 1) + b)
                        nc.tensor.matmul(y_ps[:, b, :], combT[32 * b:32 * b + E, q, :], b2_sb[32 * b:32 * b + E, :],
                                         start=True, stop=True).then_inc(s["b2_part" if b < HB - 1 else "y_full"], 1)

                def h(ep, j):
                    slot, half = j // 2 % 2, j % 2
                    if half == 0:
                        pe.wait_ge(w_e_s[slot], (tau * (E // 2) + ep + j // 4 + 1) * 48)
                    pe.wait_ge(s["sq_done"], (tau * UNITS + ep * 4 + j) * 4)
                    rows_ = slice(half * HB, (half + 1) * HB)
                    for m in range(MC):
                        for k in range(KC):
                            last = split3(h_ps[:, m, :].rearrange("p (b t) -> p b t", b=HB),
                                          w1_sb[:, slot, 0, k, m * P:(m + 1) * P], w1_sb[:, slot, 1, k, m * P:(m + 1) * P],
                                          xT_hi[:, par, k, rows_, HALO:], xT_lo[:, par, k, rows_, HALO:], k, KC)
                        last.then_inc(s["h_done"], 1)

                def turn(ep, j):
                    u = tau * UNITS + ep * 4 + j
                    pe.wait_ge(s["sq_sum"], u + 1)
                    pe.wait_ge(s["rb_sb"], FIRST + u)
                    for c in range(SUB):
                        last = nc.tensor.matmul(r_ps[:, c:c + 1], sq[:, 0, c * P:(c + 1) * P], over_hid[:, 0:1],
                                                start=True, stop=True)
                    last.then_inc(s["v_ps"], 1)
                    pe.wait_ge(s["v_rstd"], u + 1)
                    for c in range(SUB):
                        last = nc.tensor.matmul(r_ps[:, c * P:(c + 1) * P], rstd[:, c:c + 1].broadcast_to([P, P]), ident[:, :],
                                                start=True, stop=True)
                    last.then_inc(s["rb_ps"], 1)

                def y(ep, j):
                    slot, hs = j // 2 % 2, j % 2
                    pe.wait_ge(s["a_done"], (tau * UNITS + ep * 4 + j + 1) * MC)
                    pe.wait_ge(s["y_free"], tau * Y + 2 + ep * 4 + j)
                    for c in range(SUB):
                        for m in range(MC):
                            last = nc.tensor.matmul(y_ps[:, c, :], hid[:, hs, m, c * P:(c + 1) * P], w2_sb[:, slot, m, :],
                                                    start=m == 0, stop=m == MC - 1)
                    last.then_inc(s["y_full"], 1)

                pipelined(pe, lambda: h(0, 0), turn, h, y)

            def final(tau, par):
                for half in range(2):
                    i = m_fin(tau) + half * (3 + HB)
                    rows_ = slice(half * HB, (half + 1) * HB)
                    pe.wait_ge(s["m_free"], i)
                    for k in range(KC):
                        last = split3(m_ps[:, :].rearrange("p (b t) -> p b t", b=HB), wgd_hi[:, k, :], wgd_lo[:, k, :],
                                      xT_hi[:, par, k, rows_, HALO:], xT_lo[:, par, k, rows_, HALO:], k, KC)
                    last.then_inc(s["m_full"], 1)
                    for g in range(KC):
                        pe.wait_ge(s["m_free"], i + 1 + g)
                        nc.tensor.matmul(m_ps[:, :], wgu_sb[:, g * P:(g + 1) * P], gd_sb,
                                         start=True, stop=True).then_inc(s["m_full"], 1)
                    pe.wait_ge(s["og_done"], tau * 2 + half + 1)
                    for b in range(HB):
                        pe.wait_ge(s["m_free"], i + 3 + b)
                        for g in range(KC):
                            last = nc.tensor.matmul(m_ps[:, 0:D], gate_o[:, g, b * P:(b + 1) * P], wo_sb[:, g, :],
                                                    start=g == 0, stop=g == KC - 1)
                        last.then_inc(s["m_full"], 1)

            schedule(pe, prep, experts, final)

        @block.scalar
        def _(act):
            A = nc.scalar.activation
            act.wait_ge(s["setup_done"], 1)
            act.wait_ge(s["b1_ready"], 1)
            act.wait_ge(s["w1_out"], 16 * (E + 1))

            def prep(tau, par):
                for bp in range(B // 2):
                    for slot in range(2):
                        n = tau * B + bp * 2 + slot
                        act.wait_ge(x_in_s[slot], (tau * (B // 2) + bp + 1) * 16)
                        act.wait_ge(s["xstat"], n)
                        A(junk[:, :], x_in[:, slot, :], ACT.Identity, accum_out=stat[:, slot, 0:1]).then_inc(s["xsum"], 1)
                        act.wait_ge(s["xsum"], n + 1)
                        A(stat[:, slot, 1:2], stat[:, slot, 0:1], ACT.Copy, scale=-1.0 / D).then_inc(s["xneg"], 1)
                        act.wait_ge(s["xneg"], n + 1)
                        A(x_in[:, slot, :], x_in[:, slot, :], ACT.Identity, bias=stat[:, slot, 1:2]).then_inc(s["xctr"], 1)
                        act.wait_ge(s["xctr"], n + 1)
                        A(junk[:, :], x_in[:, slot, :], ACT.Square, accum_out=stat[:, slot, 2:3]).then_inc(s["xsq"], 1)
                        act.wait_ge(s["xsq"], n + 1)
                        A(stat[:, slot, 3:4], stat[:, slot, 2:3], ACT.Copy, scale=1.0 / D, bias=LN_EPS).then_inc(s["xstat"], 1)
                    for slot in range(2):
                        n = tau * B + bp * 2 + slot
                        i = m_prep(tau) + bp * 4 + slot * 2
                        b = bp * 2 + slot
                        act.wait_ge(s["xpow"], n + 1)
                        A(acc[:, par, b, :], x_in[:, slot, :], ACT.Copy, scale=stat[:, slot, 4:5]).then_inc(s["xn_ready"], 1)
                        act.wait_ge(s["m_full"], i + 1)
                        A(xT32[:, slot, :, :].rearrange("p k t -> p (k t)"), m_ps[:, 0:D], ACT.Copy)
                        A(xT_hi[:, par, :, b, HALO:],
                          m_ps[:, 0:D].rearrange("p (k t) -> p k t", k=KC), ACT.Copy).then_inc(s["m_free"], 1)
                        act.wait_ge(s["m_full"], i + 2)
                        A(logits[:, b, :], m_ps[:, 0:E], ACT.Copy).then_inc(s["m_free"], 1)
                act.wait_ge(s["y_added"], tau * Y)
                for g in range(GRP):
                    for half in range(2):
                        act.wait_ge(s["m_full"], m_prep(tau) + 2 * B + g * 2 + half + 1)
                        if not (isinstance(tau, int) and tau == 0 and g == 0):
                            act.wait_ge(qkv_out_s[half], (tau * GRP + g) * 16)
                        A(stage[:, half, :], m_ps[:, :], ACT.Silu, bias=conv_b[:, g:g + 1]).then_inc(s["m_free"], 1)
                for half in range(2):
                    act.wait_ge(s["m_full"], m_prep(tau) + 2 * B + 2 * GRP + half + 1)
                    act.wait_ge(s["ab_out"], tau * 64)
                    A(ab_stage[:, half, :], m_ps[0:2 * H, :], ACT.Sigmoid, bias=ab_b).then_inc(s["m_free"], 1)
                for n, r_ in enumerate((r_k, r_q)):
                    act.wait_ge(s["head_step"], tau * HEAD_STEPS + (6, 12)[n])
                    A(r_[:, :], head_norm[:, n, :], ACT.Abs_reciprocal_sqrt).then_inc(s["guess"], 1)

            def experts(tau, par):
                for half in range(2):
                    act.wait_ge(qkv_out_s[half], (tau + 1) * GRP * 16)
                act.wait_ge(s["ab_out"], (tau + 1) * 64)
                act.wait_ge(s["gmax"], tau + 1)
                A(expd[:, :, :].rearrange("p b e -> p (b e)"), shifted[:, :, :].rearrange("p b e -> p (b e)"),
                  ACT.Exp).then_inc(s["gexp"], 1)
                for q in range(2):
                    i = m_exp(tau) + q
                    act.wait_ge(s["m_full"], i + 1)
                    A(combT[:, q, :], m_ps[:, 0:P], ACT.Copy).then_inc(s["m_free"], 1)
                    act.wait_ge(s["y_full"], FIRST + tau * Y + q + 1)
                    act.wait_ge(s["y_added"], tau * Y + q)
                    A(y_sb[:, :, :].rearrange("p c d -> p (c d)"), y_ps[:, :, :].rearrange("p c d -> p (c d)"),
                      ACT.Copy).then_inc(s["y_free"], 1)

                def evac(ep, j):
                    u = tau * UNITS + ep * 4 + j
                    for m in range(MC):
                        act.wait_ge(s["h_done"], u * MC + m + 1)
                        A(hid[:, j % 2, m, :], h_ps[:, m, :], ACT.Identity, bias=ecol_sb[:, j // 2 % 2, 2, m:m + 1])
                        A(sq[:, m, :], h_ps[:, m, :], ACT.Square, bias=ecol_sb[:, j // 2 % 2, 2, m:m + 1]).then_inc(s["sq_done"], 1)

                def turn(ep, j):
                    u = tau * UNITS + ep * 4 + j
                    act.wait_ge(s["v_ps"], u + 1)
                    A(var_sb[:, :], r_ps[:, 0:SUB], ACT.Copy, bias=LN_EPS).then_inc(s["v_sb"], 1)
                    act.wait_ge(s["rb_ps"], u + 1)
                    A(rstd_b[:, :], r_ps[:, :], ACT.Copy).then_inc(s["rb_sb"], 1)
                    A(share[:, j, :], comb[:, par, (j % 2) * HB:(j % 2 + 1) * HB, bass.ds(ep * 2 + j // 2, 1)].rearrange(
                        "p b o -> p (b o)"), ACT.Copy)
                    for m in range(MC):
                        act.wait_ge(s["t_done"], u * MC + m + 1)
                        A(hid[:, j % 2, m, :], hid[:, j % 2, m, :], ACT.Gelu, bias=ecol_sb[:, j // 2, 1, m:m + 1],
                          scale=ecol_sb[:, j // 2, 0, m:m + 1]).then_inc(s["a_done"], 1)

                def y(ep, j):
                    n = tau * Y + 2 + ep * 4 + j
                    act.wait_ge(s["y_full"], FIRST + n + 1)
                    act.wait_ge(s["y_added"], n)
                    for c in range(SUB):
                        last = A(y_sb[:, c, :], y_ps[:, c, :], ACT.Copy, scale=share[:, j, c:c + 1])
                    last.then_inc(s["y_free"], 1)

                pipelined(act, lambda: evac(0, 0), turn, evac, y)

            def final(tau, par):
                act.wait_ge(s["y_added"], (tau + 1) * Y)
                for half in range(2):
                    i = m_fin(tau) + half * (3 + HB)
                    act.wait_ge(s["m_full"], i + 1)
                    A(gd_sb, m_ps[:, :], ACT.Silu).then_inc(s["m_free"], 1)
                    for g in range(KC):
                        act.wait_ge(s["m_full"], i + 2 + g)
                        A(gate_o[:, g, :], m_ps[:, :], ACT.Sigmoid).then_inc(s["m_free"], 1)
                    for c in range(HB):
                        b = half * HB + c
                        n = tau * B + b
                        act.wait_ge(s["z_silu"], n)
                        act.wait_ge(s["fsq"], n)
                        A(junk[:, :], acc[:, par, b, :], ACT.Identity, accum_out=fstat[:, 0:1]).then_inc(s["fsum"], 1)
                        act.wait_ge(s["fsum"], n + 1)
                        A(fstat[:, 1:2], fstat[:, 0:1], ACT.Copy, scale=-1.0 / D).then_inc(s["fneg"], 1)
                        act.wait_ge(s["fneg"], n + 1)
                        A(z, acc[:, par, b, :], ACT.Identity, bias=fstat[:, 1:2]).then_inc(s["fctr"], 1)
                        act.wait_ge(s["fctr"], n + 1)
                        A(junk[:, :], z, ACT.Square, accum_out=fstat[:, 2:3]).then_inc(s["fsum2"], 1)
                        act.wait_ge(s["fsum2"], n + 1)
                        A(fstat[:, 3:4], fstat[:, 2:3], ACT.Copy, scale=1.0 / D, bias=LN_EPS).then_inc(s["fsq"], 1)
                        act.wait_ge(s["m_full"], i + 4 + c)
                        act.wait_ge(s["res_done"], n + HAND)
                        A(s_sb[:, :], m_ps[:, 0:D], ACT.Copy).then_inc(s["m_free"], 1)
                        act.wait_ge(s["frstd"], n + 1)
                        A(z, z, ACT.Copy, scale=fstat[:, 4:5]).then_inc(s["z_norm"], 1)
                        act.wait_ge(s["z_ready"], n + 1)
                        A(z2, z, ACT.Silu).then_inc(s["z_silu"], 1)

            schedule(act, prep, experts, final)

        @block.gpsimd
        def _(pool):
            G = nc.gpsimd
            G.memset(ident[:, :], 0.0).then_inc(s["const_ready"], 1)
            G.memset(over_hid[:, :], 1.0 / HID).then_inc(s["const_ready"], 1)
            G.memset(below[:, :, :], 1.0).then_inc(s["const_ready"], 1)
            G.memset(minus_half[:, :], -0.5).then_inc(s["const_ready"], 1)
            G.memset(comb[:, :, :, :], 0.0).then_inc(s["const_ready"], 1)
            for n_, v_ in enumerate(CONSTS):
                G.memset(consts[:, n_:n_ + 1], v_).then_inc(s["const_ready"], 1)
            G.memset(combT[:, :, :], 0.0).then_inc(s["const_ready"], 1)
            pool.wait_ge(s["const_ready"], 3)
            G.affine_select(out=ident[:, :], in_=ident[:, :], compare_op=ALU.not_equal, fill=1.0, base=0,
                            pattern=[[-1, P]], channel_multiplier=1).then_inc(s["const_ready"], 1)
            G.affine_select(out=below[:, :, :], in_=below[:, :, :], compare_op=ALU.is_gt, fill=0.0, base=0,
                            pattern=[[1, E], [-1, E]], channel_multiplier=0).then_inc(s["const_ready"], 1)
            pool.wait_ge(s["w_in"], N_IN * 16)
            n = 0

            def split(hi, lo, full):
                nonlocal n
                G.tensor_copy(hi, full).then_inc(s["wsplit"], 1)
                pool.wait_ge(s["wsplit"], n + 1)
                G.tensor_tensor(lo, full, hi, ALU.subtract).then_inc(s["wsplit"], 1)
                n += 2

            for k in range(KC):
                for tap in range(TAPS):
                    pool.wait_ge(s["wsplit"], n)
                    G.tensor_tensor(wtap, wqkv_raw[:, k, :], taps_b[:, tap, :], ALU.mult).then_inc(s["wsplit"], 1)
                    n += 1
                    pool.wait_ge(s["wsplit"], n)
                    split(wp_hi[:, k, tap, :], wp_lo[:, k, tap, :], wtap)
            split(wab_hi[:, :, :], wab_lo[:, :, :], wab_raw)
            split(wgd_hi[:, :, :], wgd_lo[:, :, :], wgd_raw)
            for g in range(KC):
                G.tensor_scalar(wo_sb[:, g, :], wo_sb[:, g, :], rms_col[:, g:g + 1], None, ALU.mult).then_inc(s["wsplit"], 1)
                n += 1
            G.memset(xT_hi[:, 1, :, :, TB:], 0.0).then_inc(s["wsplit"], 1)
            G.memset(xT_lo[:, 1, :, :, TB:], 0.0).then_inc(s["wsplit"], 1)
            n += 2
            pool.wait_ge(s["wsplit"], n)
            G.memset(o_n[:, 0:1], 0.0).then_inc(s["setup_done"], 1)

            def prep(tau, par):
                for n_, part in enumerate((xT_hi, xT_lo)):
                    G.tensor_copy(part[:, par, :, :, 0:HALO], part[:, 1 - par, :, :, TB:]).then_inc(s["halo_done"], 1)
                for bp in range(B // 2):
                    for slot in range(2):
                        n = tau * B + bp * 2 + slot
                        pool.wait_ge(s["xstat"], n + 1)
                        G.tensor_tensor(stat[:, slot, 4:5], stat[:, slot, 3:4], minus_half[:, 0:1], ALU.pow).then_inc(s["xpow"], 1)
                    for slot in range(2):
                        b = bp * 2 + slot
                        pool.wait_ge(s["m_free"], m_prep(tau) + bp * 4 + slot * 2 + 1)
                        G.tensor_tensor(xT_lo[:, par, :, b, HALO:], xT32[:, slot, :, :],
                                        xT_hi[:, par, :, b, HALO:], ALU.subtract).then_inc(s["x_lo"], 1)
                hs = tau * HEAD_STEPS
                k_, q_, v_ = kq[:, par, 0, :, :], kq[:, par, 1, :, :], bv[:, par, :, :]
                t0 = [0]

                def go(ins):
                    ins.then_inc(s["head_step"], 1)
                    t0[0] += 1
                    pool.wait_ge(s["head_step"], hs + t0[0])

                def dot(out_, a_, b_):
                    go(G.tensor_tensor(head_tmp[:, :, :], a_, b_, ALU.mult))
                    w = DH // 2
                    while w > 1:
                        go(G.tensor_tensor(head_tmp[:, 0:w, :], head_tmp[:, 0:w, :], head_tmp[:, w:2 * w, :], ALU.add))
                        w //= 2
                    go(G.tensor_tensor(out_, head_tmp[:, 0, :], head_tmp[:, 1, :], ALU.add))

                def const(v, shape=(P, TB)):
                    c = CONSTS.index(v)
                    return consts[:, c:c + 1].broadcast_to(list(shape))

                def clamp(a_, v, op):
                    G.tensor_tensor(pool_spare[:, :], minus_half[:, 0:1], minus_half[:, 0:1], ALU.mult)
                    go(G.tensor_scalar(a_, a_, v, None, op))

                pool.wait_ge(s["heads_in"], (tau + 1) * 5 * 16)
                for n_, a_ in enumerate((k_, q_)):
                    dot(head_norm[:, n_, :], a_, a_)
                    clamp(head_norm[:, n_, :], NORM_MIN, ALU.max)
                dot(c_qk[:, par, :], k_, q_)
                clamp(decay[:, par, :], 0.1, ALU.max)
                clamp(decay[:, par, :], 1.0, ALU.min)
                clamp(beta[:, :], 1.0, ALU.min)
                for n_, r_ in enumerate((r_k, r_q)):
                    pool.wait_ge(s["guess"], tau * 2 + n_ + 1)
                    go(G.tensor_tensor(head_norm[:, n_, :], head_norm[:, n_, :], minus_half[:, :], ALU.mult))
                    for _ in range(3):
                        go(G.tensor_tensor(head_sq[:, :], r_[:, :], r_[:, :], ALU.mult))
                        go(G.tensor_tensor(head_sq[:, :], head_sq[:, :], head_norm[:, n_, :], ALU.mult))
                        go(G.tensor_tensor(head_sq[:, :], head_sq[:, :], const(1.5), ALU.add))
                        go(G.tensor_tensor(r_[:, :], r_[:, :], head_sq[:, :], ALU.mult))
                go(G.tensor_tensor(beta[:, :], beta[:, :], r_k[:, :], ALU.mult))
                go(G.tensor_tensor(c_v[:, par, :], beta[:, :], r_k[:, :], ALU.mult))
                go(G.tensor_tensor(c_v[:, par, :], c_v[:, par, :], const(-1.0), ALU.mult))
                go(G.tensor_tensor(v_, v_, beta[:, :].rearrange("p (o t) -> p o t", o=1).broadcast_to([P, DH, TB]), ALU.mult))
                go(G.tensor_tensor(c_q[:, par, :], decay[:, par, :], r_q[:, :], ALU.mult))
                G.tensor_tensor(c_qk[:, par, :], c_qk[:, par, :], r_q[:, :], ALU.mult).then_inc(s["heads_ready"], 1)
                assert t0[0] == HEAD_STEPS, t0[0]

            def experts(tau, par):
                def add(n, half):
                    pool.wait_ge(s["y_free"], n + 1)
                    pool.wait_ge(s["y_added"], n)
                    a_ = acc[:, par, half * HB:(half + 1) * HB, :]
                    G.tensor_tensor(a_, a_, y_sb[:, :, :], ALU.add).then_inc(s["y_added"], 1)

                for q in range(2):
                    add(tau * Y + q, q)

                def sums(ep, j):
                    u = tau * UNITS + ep * 4 + j
                    for q in range(2):
                        pool.wait_ge(s["sq_done"], u * MC + 2 * q + 2)
                        G.tensor_tensor(sq[:, 2 * q, :], sq[:, 2 * q, :], sq[:, 2 * q + 1, :], ALU.add).then_inc(s["sq_part"], 1)
                    pool.wait_ge(s["sq_part"], u * 2 + 2)
                    G.tensor_tensor(sq[:, 0, :], sq[:, 0, :], sq[:, 2, :], ALU.add).then_inc(s["sq_sum"], 1)

                def turn(ep, j):
                    u = tau * UNITS + ep * 4 + j
                    pool.wait_ge(s["v_sb"], u + 1)
                    G.tensor_tensor(rstd[:, :], var_sb[:, :], minus_half[:, 0:SUB], ALU.pow).then_inc(s["v_rstd"], 1)
                    pool.wait_ge(s["rb_sb"], FIRST + u + 1)
                    for m in range(MC):
                        G.tensor_tensor(hid[:, j % 2, m, :], hid[:, j % 2, m, :], rstd_b[:, :], ALU.mult).then_inc(s["t_done"], 1)

                def y(ep, j):
                    add(tau * Y + 2 + ep * 4 + j, j % 2)

                pipelined(pool, lambda: sums(0, 0), turn, sums, y)

            def final(tau, par):
                pool.wait_ge(s["oT_in"], (tau + 1) * 32)
                for half in range(2):
                    i = m_fin(tau) + half * (3 + HB)
                    for g in range(KC):
                        pool.wait_ge(s["m_free"], i + 2 + g)
                        last = G.tensor_tensor(gate_o[:, g, :].rearrange("p (b t) -> p b t", b=HB),
                                               gate_o[:, g, :].rearrange("p (b t) -> p b t", b=HB),
                                               oT_v[:, g, half * HB:(half + 1) * HB, :], ALU.mult)
                    last.then_inc(s["og_done"], 1)
                    for c in range(HB):
                        b = half * HB + c
                        n = tau * B + b
                        f0 = n * 2

                        def wait(k_):
                            pool.wait_ge(s["fstep"], f0 + k_)
                        pool.wait_ge(s["fsq"], n + 1)
                        G.tensor_tensor(fstat[:, 4:5], fstat[:, 3:4], minus_half[:, 0:1], ALU.pow).then_inc(s["frstd"], 1)
                        pool.wait_ge(s["z_norm"], n + 1)
                        G.tensor_tensor(z, z, rows_sb[:, 0, :], ALU.mult).then_inc(s["fstep"], 1)
                        wait(1)
                        G.tensor_tensor(z, z, rows_sb[:, 1, :], ALU.add).then_inc(s["z_ready"], 1)
                        pool.wait_ge(s["z_silu"], n + 1)
                        pool.wait_ge(s["m_free"], i + 4 + c)
                        pool.wait_ge(x_res_s[c % 2], (tau * (B // 2) + b // 2 + 1) * 16)
                        pool.wait_ge(out_s[c % 2], (tau * (B // 2) + b // 2) * 16)
                        G.tensor_tensor(z2, z2, s_sb[:, :], ALU.mult).then_inc(s["fstep"], 1)
                        wait(2)
                        G.tensor_tensor(res[:, c % 2, :], z2, x_res[:, c % 2, :], ALU.add).then_inc(s["res_done"], 1)

            schedule(pool, prep, experts, final)

        @block.vector
        def _(dve):
            V = nc.vector
            d = [0]

            def setup(ins):
                ins.then_inc(s["dsetup"], 1)
                d[0] += 1
                dve.wait_ge(s["dsetup"], d[0])

            dve.wait_ge(s["w_in"], N_IN * 16)
            dve.wait_ge(s["b1_ps"], 1)
            setup(V.tensor_reduce(b1_mean[:, :], r_ps[:, 0:E * MC].rearrange("p (e m) -> p e m", m=MC), AX, ALU.add))
            V.tensor_tensor(b1_col, b1_col,
                            b1_mean[:, :].rearrange("p (e o) -> p e o", o=1).broadcast_to([P, E, MC]),
                            ALU.subtract).then_inc(s["b1_ready"], 1)
            for e in range(E):
                for k in range(KC):
                    c = e * KC + k
                    dve.wait_ge(w1_raw_s[k], (e + 1) * 16)
                    setup(V.tensor_reduce(w_mean[:, c:c + 1], w1_raw[:, k, :], AX, ALU.add))
                    setup(V.tensor_scalar(w_mean[:, c:c + 1], w_mean[:, c:c + 1], 1.0 / HID, None, ALU.mult))
                    V.tensor_scalar(w1_ctr, w1_raw[:, k, :], w_mean[:, c:c + 1], None, ALU.subtract).then_inc(s["w1_free"], 1)
                    dve.wait_ge(s["w1_free"], c + 1)
                    if e:
                        dve.wait_ge(s["w1_out"], e * 16)
                    setup(V.tensor_copy(w1_parts[:, 0, k, :], w1_ctr))
                    if k == KC - 1:
                        V.tensor_tensor(w1_parts[:, 1, k, :], w1_ctr, w1_parts[:, 0, k, :], ALU.subtract).then_inc(s["w1_split"], 1)
                        dve.wait_ge(s["w1_split"], e + 1)
                    else:
                        setup(V.tensor_tensor(w1_parts[:, 1, k, :], w1_ctr, w1_parts[:, 0, k, :], ALU.subtract))
            setup(V.memset(state[:, 0, :, :], 0.0))
            dve.wait_ge(s["setup_done"], 1)
            dve.wait_ge(s["const_ready"], N_CONST)

            def gating(tau, par):
                gs = tau * GATE_STEPS
                n = [0]

                def go(ins):
                    ins.then_inc(s["dgate"], 1)
                    n[0] += 1
                    dve.wait_ge(s["dgate"], gs + n[0])

                def bc(ap, shape, where):
                    return ap.rearrange(where, o=1).broadcast_to(shape)

                full = [P, B, E, E]
                dve.wait_ge(s["m_free"], m_prep(tau) + 2 * B)
                go(V.tensor_reduce(lmax[:, :], logits[:, :, :], AX, ALU.max))
                V.tensor_tensor(shifted[:, :, :], logits[:, :, :], bc(lmax[:, :], [P, B, E], "p (b o) -> p b o"),
                                ALU.subtract).then_inc(s["gmax"], 1)
                dve.wait_ge(s["gmax"], tau + 1)
                other = bc(shifted[:, :, :], full, "p (b o) f -> p b o f") if False else \
                    shifted[:, :, :].rearrange("p b (o f) -> p b o f", o=1).broadcast_to(full)
                own = shifted[:, :, :].rearrange("p b (e o) -> p b e o", o=1).broadcast_to(full)
                go(V.tensor_tensor(cmp_gt[:, :, :, :], other, own, ALU.is_gt))
                go(V.tensor_tensor(cmp_eq[:, :, :, :], other, own, ALU.is_equal))
                go(V.tensor_tensor(cmp_eq[:, :, :, :], cmp_eq[:, :, :, :],
                                   below[:, :, :].rearrange("p (o e) f -> p o e f", o=1).broadcast_to(full), ALU.mult))
                go(V.tensor_tensor(cmp_gt[:, :, :, :], cmp_gt[:, :, :, :], cmp_eq[:, :, :, :], ALU.add))
                go(V.tensor_reduce(rank[:, :, :], cmp_gt[:, :, :, :], AX, ALU.add))
                go(V.tensor_scalar(rank[:, :, :], rank[:, :, :], 1.5, None, ALU.is_lt))
                dve.wait_ge(s["gexp"], tau + 1)
                go(V.tensor_tensor(rank[:, :, :], rank[:, :, :], expd[:, :, :], ALU.mult))
                go(V.tensor_reduce(csum[:, :], rank[:, :, :], AX, ALU.add))
                go(V.reciprocal(csum[:, :], csum[:, :]))
                dve.wait_ge(s["o_out"], 16 * FIRST + tau * 16)
                V.tensor_tensor(comb[:, par, :, 0:E], rank[:, :, :], bc(csum[:, :], [P, B, E], "p (b o) -> p b o"),
                                ALU.mult).then_inc(s["comb_ready"], 1)
                assert n[0] == GATE_STEPS, n[0]

            def recurrence(tau, par):
                dve.wait_ge(s["heads_ready"], tau + 1)
                gating(tau, par)
                k_all, q_all = kq[:, par, 0, :, :], kq[:, par, 1, :, :]
                with dve.Fori(0, NG) as grp:
                    base = (tau * NG + grp) * GROUP_STEPS
                    n = [0]

                    def do(ins):
                        ins.then_inc(s["step"], 1)
                        n[0] += 1
                        return n[0]

                    def done(k_):
                        dve.wait_ge(s["step"], FIRST + base + k_)

                    for i in range(GT):
                        t = bass.ds(grp * GT + i, 1)
                        S_in, S_out = state[:, i % 2, :, :], state[:, (i + 1) % 2, :, :]
                        k_t = k_all[:, :, t].rearrange("p i o -> p o i").broadcast_to([P, DH, DH])
                        q_t = q_all[:, :, t].rearrange("p i o -> p o i")
                        hw = DH // 2
                        done(n[0])
                        a1 = do(V.tensor_tensor(prod_k[:, :, :], S_in, k_t, ALU.mult))
                        do(V.tensor_tensor(prod_q[:, 0:hw, :], S_in[:, 0:hw, :], q_t.broadcast_to([P, hw, DH]), ALU.mult))
                        done(a1)
                        a3 = do(V.tensor_reduce(ks[:, :], prod_k[:, :, :], AX, ALU.add))
                        a4 = do(V.tensor_tensor(prod_q[:, hw:, :], S_in[:, hw:, :], q_t.broadcast_to([P, hw, DH]), ALU.mult))
                        done(a3)
                        a5 = do(V.scalar_tensor_tensor(out=upd[:, i, :], in0=ks[:, :], scalar=c_v[:, par, t],
                                                       in1=bv[:, par, :, t].rearrange("p j o -> p (j o)"),
                                                       op0=ALU.mult, op1=ALU.add))
                        do(V.tensor_reduce(qs[:, i, 0:hw], prod_q[:, 0:hw, :], AX, ALU.add))
                        done(a5)
                        a7 = do(V.tensor_tensor(outer[:, :, :],
                                                upd[:, i, :].rearrange("p (j o) -> p j o", o=1).broadcast_to([P, DH, DH]),
                                                k_t, ALU.mult))
                        a8 = do(V.tensor_reduce(qs[:, i, hw:], prod_q[:, hw:, :], AX, ALU.add))
                        done(a7)
                        do(V.scalar_tensor_tensor(out=S_out, in0=S_in, scalar=decay[:, par, t], in1=outer[:, :, :],
                                                  op0=ALU.mult, op1=ALU.add))
                    ts_ = bass.ds(grp * GT, GT)

                    def per_token(ap):
                        return ap[:, par, ts_].rearrange("p (t o) -> p t o", o=1).broadcast_to([P, GT, DH])

                    o_view = o_all[:, :, ts_].rearrange("p j t -> p t j")
                    done(n[0])
                    b1 = do(V.tensor_tensor(o_t1[:, :, :], qs[:, :, :], per_token(c_q), ALU.mult))
                    b2_ = do(V.tensor_tensor(o_t2[:, :, :], upd[:, :, :], per_token(c_qk), ALU.mult))
                    done(b2_)
                    b3 = do(V.tensor_tensor(o_view, o_t1[:, :, :], o_t2[:, :, :], ALU.add))
                    done(b3)
                    b4 = do(V.tensor_tensor(o_sq[:, :, :], o_view, o_view, ALU.mult))
                    done(b4)
                    b5 = do(V.tensor_reduce(o_ms[:, ts_], o_sq[:, :, :], AX, ALU.add))
                    done(b5)
                    assert n[0] == GROUP_STEPS, n[0]
                bs = tau * BLOCK_STEPS
                n = [0]

                def go(ins):
                    ins.then_inc(s["block_step"], 1)
                    n[0] += 1
                    dve.wait_ge(s["block_step"], bs + n[0])

                go(V.tensor_scalar(o_ms[:, :], o_ms[:, :], 1.0 / DH, RMS_EPS, ALU.mult, ALU.add))
                go(V.tensor_scalar(o_r[:, :].bitcast(I32), o_ms[:, :].bitcast(I32), -0.5, MAGIC, ALU.mult, ALU.add))
                for _ in range(3):
                    go(V.scalar_tensor_tensor(out=o_n[:, :], in0=o_r[:, :], scalar=-0.5, in1=o_r[:, :], op0=ALU.mult, op1=ALU.mult))
                    go(V.tensor_tensor(o_n[:, :], o_n[:, :], o_ms[:, :], ALU.mult))
                    go(V.scalar_tensor_tensor(out=o_r[:, :], in0=o_n[:, :], scalar=1.5, in1=o_r[:, :], op0=ALU.add, op1=ALU.mult))
                V.tensor_tensor(o_all[:, :, :], o_all[:, :, :],
                                o_r[:, :].rearrange("p (o t) -> p o t", o=1).broadcast_to([P, DH, TB]),
                                ALU.mult).then_inc(s["o_ready"], 1)
                assert n[0] == BLOCK_STEPS, n[0]

            with dve.Fori(0, NB // 2) as m:
                for par in range(2):
                    recurrence_tau = m * 2 + par
                    recurrence(recurrence_tau, par)


def kernel(**inputs):
    import numpy as np
    import concourse.bacc as bacc
    from concourse.bass_utils import run_bass_kernel_spmd

    a = {k[3:]: np.asarray(v) for k, v in inputs.items()}
    f = {k[5:] if k.startswith("attn_") else k[4:] + "_f": v for k, v in a.items()}

    def by_partition(v, chunks):
        return v.reshape(chunks, P).T

    ab = np.zeros((P, 1), np.float32)
    ab[0:H, 0], ab[H:2 * H, 0] = f["ba"], f["bb"]
    cols = np.concatenate(
        [by_partition(f[n], KC) for n in ("qcb", "kcb", "vcb")] + [ab, by_partition(f["rms_w"].reshape(-1), KC)]
        + [by_partition(f[n][e], MC) for e in range(E) for n in ("ln1_g_f", "ln1_b_f", "b1_f")], axis=1)
    arrays = {
        "x": f["x"],
        "wqkv": np.concatenate([f["Wq"], f["Wk"], f["Wv"]], axis=1),
        "cw": np.concatenate([f["qcw"], f["kcw"], f["vcw"]], axis=0).T,
        "wab": np.concatenate([f["Wa"], f["Wb"]], axis=1),
        "wgd": f["Wgd"], "wgu": f["Wgu"], "wo": f["Wo"], "gate": f["gate_w_f"],
        "w1": f["w1_f"], "w2": f["w2_f"], "b2": f["b2_f"],
        "rows": np.stack([f["ln_g_f"], f["ln_b_f"]]),
        "cols": cols,
    }
    nc = bacc.Bacc("TRN2", target_bir_lowering=False, num_devices=1)
    maps, args = {}, []
    for name, v in arrays.items():
        v = np.ascontiguousarray(v)
        maps[f"in_{name}"] = v
        args.append(nc.dram_tensor(f"in_{name}", v.shape, mybir.dt.from_np(v.dtype), kind="ExternalInput").ap())
    out = nc.dram_tensor("out_0", f["x"].shape, F32, kind="ExternalOutput").ap()
    bass_delta_moe(nc, *args, out)
    r = run_bass_kernel_spmd(nc, [maps], core_ids=[0])
    return r.results[0]["out_0"]
```

```python
from contextlib import ExitStack

import concourse.bass as bass
from concourse import mybir

F32 = mybir.dt.float32
F16 = mybir.dt.float16
I32 = mybir.dt.int32
ALU = mybir.AluOpType
ACT = mybir.ActivationFunctionType
AX = mybir.AxisListType.X

P = 128
B, T, D = 8, 1024, 256
H, DH = 16, 16
E, HID = 8, 512
TB = 128
NB = T // TB
KC = D // P
MC = HID // P
TAPS = 4
HALO = TAPS - 1
GRP = 3 * KC
HB = B // 2
HT = HB * TB
SUB = HT // P
XS = 4
UNITS = 2 * E
GT = 8
NG = TB // GT
STEP = 9
LN_EPS = 1e-5
RMS_EPS = 1e-6
NORM_MIN = 1e-12
HEAD_STEPS = 3 * 2 + 2 + 3 * 3 + 6
GATE_STEPS = 10
OUT_STEPS = 3
GROUP_STEPS = GT * STEP + OUT_STEPS
BLOCK_STEPS = 4 + 3 * 3
MAGIC = float(0x5F3759DF)


def bass_delta_moe(nc, x, wqkv, cw, wab, wgd, wgu, wo, gate, w1, w2, b2, rows, cols, out):
    ctx = ExitStack()
    with ctx:
        def sb(name, shape, dt=F32):
            return ctx.enter_context(nc.sbuf_tensor(name, shape, dt))

        def ps(name, shape):
            return ctx.enter_context(nc.psum_tensor(name, shape, F32))

        def sem(name):
            return ctx.enter_context(nc.semaphore(name))

        qkv_dram = nc.dram_tensor("qkv_scratch", (2, 3, B, H * DH, TB), F32, kind="Internal").ap()
        ab_dram = nc.dram_tensor("ab_scratch", (2, 2, B, H, TB), F32, kind="Internal").ap()
        o_dram = nc.dram_tensor("o_scratch", (2, B, H * DH, TB), F32, kind="Internal").ap()
        ecol_dram = nc.dram_tensor("ecol_scratch", (E, P, 3 * MC), F32, kind="Internal").ap()
        w1_dram = nc.dram_tensor("w1_scratch", (E, P, 2 * KC * HID), F16, kind="Internal").ap()

        ident = sb("ident", [P, P])
        over_hid = sb("over_hid", [P, P])
        below = sb("below", [P, E, E])
        minus_half = sb("minus_half", [P, P])
        wp_hi = sb("wp_hi", [P, KC, TAPS, 3 * D], F16)
        wp_lo = sb("wp_lo", [P, KC, TAPS, 3 * D], F16)
        wab_hi = sb("wab_hi", [P, KC, 2 * H], F16)
        wab_lo = sb("wab_lo", [P, KC, 2 * H], F16)
        wgd_hi = sb("wgd_hi", [P, KC, P], F16)
        wgd_lo = sb("wgd_lo", [P, KC, P], F16)
        wgu_sb = sb("wgu_sb", [P, D])
        wo_sb = sb("wo_sb", [P, KC, D])
        gate_sb = sb("gate_sb", [P, KC, E])
        b2_sb = sb("b2_sb", [P, D])
        rows_sb = sb("rows_sb", [P, 2, D])
        NCOL = cols.shape[1]
        cols_sb = sb("cols_sb", [P, NCOL])
        conv_b = cols_sb[:, 0:GRP]
        ab_b = cols_sb[0:2 * H, GRP:GRP + 1]
        rms_col = cols_sb[:, GRP + 1:GRP + 1 + KC]
        ECOL = 3 * MC
        expert_cols = cols_sb[:, GRP + 3:GRP + 3 + E * ECOL].rearrange("p (e n m) -> p e n m", e=E, n=3)
        b1_col = expert_cols[:, :, 2, :]
        b1_mean = sb("b1_mean", [P, E])
        w_mean = sb("w_mean", [P, E * KC])

        x_in = sb("x_in", [P, XS, D])
        junk = sb("junk", [P, D])
        stat = sb("stat", [P, XS, 6])
        acc = sb("acc", [P, 2, B, D])
        xT_hi = sb("xT_hi", [P, 2, KC, B, HALO + TB], F16)
        xT_lo = sb("xT_lo", [P, 2, KC, B, HALO + TB], F16)
        logits = sb("logits", [P, B, E])
        lmax = sb("lmax", [P, B])
        shifted = sb("shifted", [P, B, E])
        expd = sb("expd", [P, B, E])
        rank = sb("rank", [P, B, E])
        csum = sb("csum", [P, B])
        comb = sb("comb", [P, 2, B, 32])
        combT = sb("combT", [P, 2, P])

        kq = sb("kq", [P, 2, 2, DH, TB])
        bv = sb("bv", [P, 2, DH, TB])
        decay = sb("decay", [P, 2, TB])
        beta = sb("beta", [P, TB])
        c_v = sb("c_v", [P, 2, TB])
        c_q = sb("c_q", [P, 2, TB])
        c_qk = sb("c_qk", [P, 2, TB])
        head_tmp = sb("head_tmp", [P, DH, TB])
        head_norm = sb("head_norm", [P, 2, TB])
        head_sq = sb("head_sq", [P, 2, TB])
        r_kq = sb("r_kq", [P, 2, TB])
        state = sb("state", [P, 2, DH, DH])
        prod_k = sb("prod_k", [P, DH, DH])
        prod_q = sb("prod_q", [P, DH, DH])
        outer = sb("outer", [P, DH, DH])
        cmp_gt = prod_k[:, :, :].rearrange("p a b -> p (a b)").bitcast(F16).rearrange("p (b e f) -> p b e f", b=B, e=E)
        cmp_eq = outer[:, :, :].rearrange("p a b -> p (a b)").bitcast(F16).rearrange("p (b e f) -> p b e f", b=B, e=E)
        ks = sb("ks", [P, DH])
        qs = sb("qs", [P, GT, DH])
        upd = sb("upd", [P, GT, DH])
        o_t1 = sb("o_t1", [P, GT, DH])
        o_t2 = sb("o_t2", [P, GT, DH])
        o_ms = sb("o_ms", [P, TB])
        o_r = sb("o_r", [P, TB])
        o_n = sb("o_n", [P, TB])

        w1_sb = sb("w1_sb", [P, 2, 2, KC, HID], F16)
        w2_sb = sb("w2_sb", [P, 2, MC, D])
        ecol_sb = sb("ecol_sb", [P, 2, 3, MC])
        share = sb("share", [P, 4, HB])
        hid = sb("hid", [P, 3, MC, HT])
        RAW = 2
        sq = sb("sq", [P, MC, HT])
        var_sb = sb("var_sb", [P, SUB])
        rstd = sb("rstd", [P, SUB])
        rstd_b = sb("rstd_b", [P, HT])
        y_sb = sb("y_sb", [P, SUB, D])

        oT_v = hid[:, RAW, :, :].rearrange("p m (b t) -> p (m b) t", t=TB).rearrange("p (g b) t -> p g b t", g=KC)
        z = hid[:, 1, 1, :].rearrange("p (s d) -> p s d", s=2)
        z2 = hid[:, 1, 2, :].rearrange("p (s d) -> p s d", s=2)
        s_sb = hid[:, 1, 3, :].rearrange("p (s d) -> p s d", s=2)
        x_res = sb("x_res", [P, 2, D])
        fstat = sb("fstat", [P, 2, 6])
        gate_o = sq[:, 0:KC, :]
        gd_sb = sq[:, KC, :]
        stage = y_sb[:, :, :].rearrange("p c d -> p (c d)").rearrange("p (s t) -> p s t", s=2)
        ab_stage = hid[0:2 * H, 0, 0:2, :]
        xT32 = hid[:, 1, 0, :].rearrange("p (s k t) -> p s k t", s=2, k=KC)
        res = sb("res", [P, 2, D])

        h_ps = ps("h_ps", [P, MC, HT])
        y_ps = ps("y_ps", [P, SUB, D])
        r_ps = ps("r_ps", [P, HT])
        m_ps = ps("m_ps", [P, HT])


        names = """w_in w1_raw0 w1_raw1 w1_free w1_split w1_out const_ready wsplit setup_done
        b1_ps b1_ready dsetup
        x_in0 x_in1 x_in2 x_in3 xctr xsum xsq xneg xstat xpow xn_ready x_lo halo_done m_full m_free
        qkv_out0 qkv_out1 ab_out heads_in head_step gmax gexp comb_ready dgate
        step block_step o_ready o_out
        w1_e0 w1_e1 w2_e0 w2_e1 h_done sq_done sq_part sq_sum v_ps v_sb v_rstd rb_ps rb_sb t_done a_done
        b2_part y_full y_free y_added
        oT_in og_done fsum fsum2 fneg fctr frstd z_norm fsq fstep z_ready z_silu res_done x_res0 x_res1 out0 out1""".split()
        s = {n: sem(n) for n in names}
        x_in_s = [s[f"x_in{i}"] for i in range(XS)]
        qkv_out_s = (s["qkv_out0"], s["qkv_out1"])
        w1_e_s = (s["w1_e0"], s["w1_e1"])
        w2_e_s = (s["w2_e0"], s["w2_e1"])
        x_res_s = (s["x_res0"], s["x_res1"])
        out_s = (s["out0"], s["out1"])
        w1_raw_s = (s["w1_raw0"], s["w1_raw1"])
        HAND = 2
        FIRST = 1
        AHEAD = 2 * MC + 1
        N_CONST = 8
        N_IN = 13

        M_PREP, M_EXP, M_FIN = 2 * B + 2 * GRP + 2, 2, 2 * (3 + HB)

        def m_prep(tau):
            return 0 if isinstance(tau, int) and tau == 0 else tau * (M_PREP + M_EXP) + (tau - 1) * M_FIN

        def m_exp(tau):
            return (tau + 1) * M_PREP + tau * (M_EXP + M_FIN)

        def m_fin(tau):
            n_prep = NB if isinstance(tau, int) and tau == NB - 1 else tau + 2
            n_exp = NB if isinstance(tau, int) and tau == NB - 1 else tau + 2
            return n_prep * M_PREP + (tau + 1) * M_EXP + tau * M_FIN

        Y = 2 + UNITS

        taps_b = hid[:, :, :, :].rearrange("p a m t -> p (a m t)")[:, 0:TAPS * 3 * D].rearrange(
            "p (k c) -> p k c", k=TAPS)
        wqkv_raw = sq[:, :, :].rearrange("p m t -> p (m t)")[:, 0:KC * 3 * D].rearrange("p (k c) -> p k c", k=KC)
        wtap = head_tmp[:, :, :].rearrange("p a b -> p (a b)")[:, 0:3 * D]
        small_raw = x_res[:, :, :].rearrange("p s d -> p (s d)")
        wgd_raw = small_raw[:, 0:KC * P].rearrange("p (k c) -> p k c", k=KC)
        wab_raw = small_raw[:, KC * P:KC * P + KC * 2 * H].rearrange("p (k c) -> p k c", k=KC)
        w1_raw = y_sb[:, :, :].rearrange("p a b -> p (a b)").rearrange("p (s h) -> p s h", s=2)
        w1_ctr = res[:, :, :].rearrange("p s d -> p (s d)")
        w1_parts = w1_sb[:, 0, :, :, :]

        block = ctx.enter_context(nc.Block())

        def schedule(eng, prep, experts, final):
            prep(0, 0)
            experts(0, 0)
            prep(1, 1)
            with eng.Fori(0, (NB - 2) // 2) as m:
                for j in range(2):
                    tau = m * 2 + (j + 1)
                    final(tau - 1, j % 2)
                    experts(tau, (j + 1) % 2)
                    prep(tau + 1, j % 2)
            final(NB - 2, 0)
            experts(NB - 1, 1)
            final(NB - 1, 1)

        def pipelined(first, turn, last):
            def of(eng):
                first()
                turn(0, 0)
                with eng.Fori(0, E // 2 - 1) as ep:
                    for j in range(1, 5):
                        turn(ep, j)
                for j in range(1, 4):
                    turn(E // 2 - 1, j)
                last()
            return of

        def tile_of(dram, tau, b):
            return dram[bass.ds(b, 1), bass.ds(tau * TB, TB), :].rearrange("o t d -> (o t) d")

        @block.sync
        def _(sp):
            sp.sem_inc(s["xn_ready"], XS)
            sp.sem_inc(s["res_done"], HAND)
            sp.sem_inc(s["z_silu"], HAND)
            sp.sem_inc(s["step"], FIRST + OUT_STEPS)
            for t_ in ("y_full", "rb_sb", "fsq"):
                sp.sem_inc(s[t_], FIRST)
            for o_ in out_s:
                sp.sem_inc(o_, 16 * FIRST)
            for t_ in ("h_done", "a_done"):
                sp.sem_inc(s[t_], AHEAD)
            sp.dma_start(cols_sb[:, :], cols).then_inc(s["w_in"], 16)
            sp.dma_start(rows_sb[:, :, :], rows.rearrange("(o r) d -> o r d", o=1).broadcast_to([P, 2, D])).then_inc(s["w_in"], 16)
            sp.dma_start(taps_b, cw.rearrange("(o k) c -> o k c", o=1).broadcast_to([P, TAPS, 3 * D])).then_inc(s["w_in"], 16)
            sp.dma_start(wqkv_raw, wqkv.rearrange("(k p) c -> p k c", p=P)).then_inc(s["w_in"], 16)
            sp.dma_start(wgd_raw, wgd.rearrange("(k p) c -> p k c", p=P)).then_inc(s["w_in"], 16)
            sp.dma_start(wab_raw, wab.rearrange("(k p) c -> p k c", p=P)).then_inc(s["w_in"], 16)
            sp.dma_start(wgu_sb[:, :], wgu).then_inc(s["w_in"], 16)
            sp.dma_start(wo_sb[:, :, :], wo.rearrange("(k p) c -> p k c", p=P)).then_inc(s["w_in"], 16)
            sp.dma_start(gate_sb[:, :, :], gate.rearrange("(k p) c -> p k c", p=P)).then_inc(s["w_in"], 16)
            for q in range(4):
                sp.dma_start(b2_sb[32 * q:32 * q + E, :], b2).then_inc(s["w_in"], 16)
            for e in range(E):
                for k in range(KC):
                    if e > 0:
                        sp.wait_ge(s["w1_free"], (e - 1) * KC + k + 1)
                    sp.dma_start(w1_raw[:, k, :], w1[e, k * P:(k + 1) * P, :]).then_inc(w1_raw_s[k], 16)
                sp.wait_ge(s["w1_split"], e + 1)
                sp.dma_start(w1_dram[e], w1_parts.rearrange("p h k c -> p (h k c)")).then_inc(s["w1_out"], 16)
            sp.wait_ge(s["b1_ready"], 1)
            sp.dma_start(ecol_dram.rearrange("e p c -> p e c"),
                         expert_cols.rearrange("p e n m -> p e (n m)")).then_inc(s["w1_out"], 16)
            sp.wait_ge(s["w1_out"], 16 * (E + 1))

            def fetch_outputs(tau, par):
                sp.wait_ge(s["o_ready"], tau + 1)
                sp.dma_start(o_dram[par].rearrange("b (h j) t -> (b h) (j t)", h=H),
                             kq[:, par, 1, :, :].rearrange("p j t -> p (j t)")).then_inc(s["o_out"], 16)
                sp.wait_ge(s["o_out"], (tau + 1) * 16)
                for g in range(KC):
                    sp.dma_start(oT_v[:, g, :, :],
                                 o_dram[par].rearrange("b (g c) t -> g c b t", g=KC)[g]).then_inc(s["oT_in"], 16)

            def prep(tau, par):
                with sp.Fori(0, B // XS) as bp:
                    for slot in range(XS):
                        b = bp * XS + slot
                        sp.wait_ge(s["xn_ready"], tau * B + b + 1)
                        sp.dma_start(x_in[:, slot, :], tile_of(x, tau, b)).then_inc(x_in_s[slot], 16)
                for g in range(GRP):
                    for half in range(2):
                        sp.wait_ge(s["m_free"], m_prep(tau) + 2 * B + g * 2 + half + 1)
                        dst = qkv_dram[par, g // KC, half * HB:(half + 1) * HB, (g % KC) * P:(g % KC + 1) * P, :]
                        sp.dma_start(dst.rearrange("b c t -> c b t"),
                                     stage[:, half, :].rearrange("p (b t) -> p b t", b=HB)).then_inc(qkv_out_s[half], 16)
                for half in range(2):
                    sp.wait_ge(s["m_free"], m_prep(tau) + 2 * B + 2 * GRP + half + 1)
                    for which in range(2):
                        dst = ab_dram[par, which, half * HB:(half + 1) * HB, :, :]
                        sp.dma_start(dst.rearrange("b h t -> h b t"),
                                     ab_stage[which * H:(which + 1) * H, half, :].rearrange("p (b t) -> p b t", b=HB)).then_inc(s["ab_out"], 16)
                if not (isinstance(tau, int) and tau == 0):
                    fetch_outputs(tau - 1, 1 - par)
                for half in range(2):
                    sp.wait_ge(qkv_out_s[half], (tau + 1) * GRP * 16)
                sp.wait_ge(s["ab_out"], (tau + 1) * 4 * 16)
                if not (isinstance(tau, int) and tau < 2):
                    sp.wait_ge(s["o_ready"], tau - 1)
                if not (isinstance(tau, int) and tau < 1):
                    sp.wait_ge(s["head_step"], tau * HEAD_STEPS - 2)
                for src, dst in ((1, kq[:, par, 0, :, :]), (0, kq[:, par, 1, :, :]), (2, bv[:, par, :, :])):
                    sp.dma_start(dst.rearrange("p d t -> p (d t)"),
                                 qkv_dram[par, src].rearrange("b (h d) t -> (b h) (d t)", h=H)).then_inc(s["heads_in"], 16)
                for which, dst in ((0, decay[:, par, :]), (1, beta[:, :])):
                    sp.dma_start(dst, ab_dram[par, which].rearrange("b h t -> (b h) t")).then_inc(s["heads_in"], 16)

            def experts(tau, par):
                with sp.Fori(0, E // 2) as ep:
                    for slot in range(2):
                        e = ep * 2 + slot
                        before = (tau * UNITS + ep * 4 + (slot * 2 - 2)) * MC
                        sp.wait_ge(s["h_done"], before + AHEAD)
                        sp.dma_start(w1_sb[:, slot, :, :, :].rearrange("p h k c -> p (h k c)"),
                                     w1_dram[bass.ds(e, 1)].rearrange("o p c -> (o p) c")).then_inc(w1_e_s[slot], 16)
                        sp.wait_ge(s["a_done"], before + AHEAD)
                        sp.dma_start(ecol_sb[:, slot, :, :].rearrange("p n m -> p (n m)"),
                                     ecol_dram[bass.ds(e, 1)].rearrange("o p c -> (o p) c")).then_inc(w1_e_s[slot], 16)
                        sp.wait_ge(s["y_full"], FIRST + tau * Y + ep * 4 + slot * 2)
                        sp.dma_start(w2_sb[:, slot, :, :],
                                     w2[bass.ds(e, 1)].rearrange("o (m p) d -> p (o m) d", p=P)).then_inc(w2_e_s[slot], 16)

            def final(tau, par):
                if isinstance(tau, int) and tau == NB - 1:
                    sp.wait_ge(s["t_done"], NB * UNITS * MC)
                    fetch_outputs(tau, par)
                with sp.Fori(0, B // 2) as bp:
                    for slot in range(2):
                        b = bp * 2 + slot
                        sp.wait_ge(s["res_done"], tau * B + b + 1)
                        sp.dma_start(x_res[:, slot, :], tile_of(x, tau, b)).then_inc(x_res_s[slot], 16)
                    for slot in range(2):
                        b = bp * 2 + slot
                        sp.wait_ge(s["res_done"], tau * B + b + HAND + 1)
                        sp.dma_start(tile_of(out, tau, b), res[:, slot, :]).then_inc(out_s[slot], 16)

            schedule(sp, prep, experts, final)
            for q in range(2):
                sp.wait_ge(out_s[q], (FIRST + NB * (B // 2)) * 16)

        @block.tensor
        def _(pe):
            def split3(out_, w_hi, w_lo, x_hi, x_lo, n, of):
                parts = ((w_hi, x_hi), (w_hi, x_lo), (w_lo, x_hi))
                for i, (a_, b_) in enumerate(parts):
                    last = nc.tensor.matmul(out_, a_, b_, start=(n == 0 and i == 0), stop=(n == of - 1 and i == 2))
                return last

            pe.wait_ge(s["const_ready"], N_CONST)
            pe.wait_ge(s["w_in"], N_IN * 16)
            nc.tensor.matmul(r_ps[:, 0:E * MC].rearrange("p (e m) -> p e m", m=MC), over_hid[:, :], b1_col, start=True, stop=True).then_inc(s["b1_ps"], 1)
            pe.wait_ge(s["setup_done"], 1)
            pe.wait_ge(s["b1_ready"], 1)

            def prep(tau, par):
                slots_ = (m_ps, r_ps)
                for bp in range(B // 2):
                    for slot in range(2):
                        i = m_prep(tau) + bp * 4 + slot
                        pe.wait_ge(s["xn_ready"], tau * B + bp * 2 + slot + XS + 1)
                        pe.wait_ge(s["m_free"], i - (1 if bp else slot))
                        for k in range(KC):
                            last = nc.tensor.transpose(slots_[slot][:, k * P:(k + 1) * P],
                                                       acc[:, par, bp * 2 + slot, k * P:(k + 1) * P], ident[:, :])
                        last.then_inc(s["m_full"], 1)
                    for slot in range(2):
                        pe.wait_ge(s["m_free"], m_prep(tau) + bp * 4 + slot + 1)
                        for k in range(KC):
                            last = nc.tensor.matmul(slots_[slot][:, 0:E], xT32[:, slot, k, :], gate_sb[:, k, :],
                                                    start=k == 0, stop=k == KC - 1)
                        last.then_inc(s["m_full"], 1)
                pe.wait_ge(s["x_lo"], (tau + 1) * B)
                pe.wait_ge(s["halo_done"], (tau + 1) * 2)
                for g in range(GRP):
                    for half in range(2):
                        pe.wait_ge(s["m_free"], m_prep(tau) + 2 * B + g * 2 + half - 1)
                        o_ = slots_[half][:, :].rearrange("p (b t) -> p b t", b=HB)
                        for n in range(KC * TAPS):
                            k, tap = n // TAPS, n % TAPS
                            rows_ = slice(half * HB, (half + 1) * HB)
                            last = split3(o_, wp_hi[:, k, tap, g * P:(g + 1) * P], wp_lo[:, k, tap, g * P:(g + 1) * P],
                                          xT_hi[:, par, k, rows_, tap:tap + TB], xT_lo[:, par, k, rows_, tap:tap + TB],
                                          n, KC * TAPS)
                        last.then_inc(s["m_full"], 1)
                for half in range(2):
                    pe.wait_ge(s["m_free"], m_prep(tau) + 2 * B + 2 * GRP + half - 1)
                    o_ = slots_[half][0:2 * H, :].rearrange("p (b t) -> p b t", b=HB)
                    for k in range(KC):
                        rows_ = slice(half * HB, (half + 1) * HB)
                        last = split3(o_, wab_hi[:, k, :], wab_lo[:, k, :], xT_hi[:, par, k, rows_, HALO:],
                                      xT_lo[:, par, k, rows_, HALO:], k, KC)
                    last.then_inc(s["m_full"], 1)

            def experts(tau, par):
                pe.wait_ge(s["comb_ready"], tau + 1)
                for q in range(2):
                    i = m_exp(tau) + q
                    pe.wait_ge(s["m_free"], i)
                    nc.tensor.transpose(m_ps[:, 0:P], comb[:, par, q * HB:(q + 1) * HB, :].rearrange("p b c -> p (b c)"),
                                        ident[:, :]).then_inc(s["m_full"], 1)
                    pe.wait_ge(s["m_free"], i + 1)
                    pe.wait_ge(s["y_free"], tau * Y + q)
                    for b in range(HB):
                        if b > 0:
                            pe.wait_ge(s["b2_part"], (tau * 2 + q) * (HB - 1) + b)
                        nc.tensor.matmul(y_ps[:, b, :], combT[32 * b:32 * b + E, q, :], b2_sb[32 * b:32 * b + E, :],
                                         start=True, stop=True).then_inc(s["b2_part" if b < HB - 1 else "y_full"], 1)

                def h(ep, j, chunks):
                    slot, half = j // 2 % 2, j % 2
                    if half == 0 and 0 in chunks:
                        pe.wait_ge(w1_e_s[slot], (tau * (E // 2) + ep + j // 4 + 1) * 32)
                    if 0 in chunks:
                        pe.wait_ge(s["sq_done"], (tau * UNITS + ep * 4 + j) * MC)
                    rows_ = slice(half * HB, (half + 1) * HB)
                    for m in chunks:
                        for k in range(KC):
                            last = split3(h_ps[:, m, :].rearrange("p (b t) -> p b t", b=HB),
                                          w1_sb[:, slot, 0, k, m * P:(m + 1) * P], w1_sb[:, slot, 1, k, m * P:(m + 1) * P],
                                          xT_hi[:, par, k, rows_, HALO:], xT_lo[:, par, k, rows_, HALO:], k, KC)
                        last.then_inc(s["h_done"], 1)

                def turn(ep, j):
                    u = tau * UNITS + ep * 4 + j
                    pe.wait_ge(s["sq_sum"], u + 1)
                    pe.wait_ge(s["rb_sb"], FIRST + u)
                    for c in range(SUB):
                        last = nc.tensor.matmul(r_ps[:, c:c + 1], sq[:, 0, c * P:(c + 1) * P], over_hid[:, 0:1],
                                                start=True, stop=True)
                    last.then_inc(s["v_ps"], 1)
                    more = not (isinstance(ep, int) and ep * 4 + j == UNITS - 1)
                    if more:
                        h(ep, j + 1, range(0, 1))
                    pe.wait_ge(s["v_rstd"], u + 1)
                    for c in range(SUB):
                        last = nc.tensor.matmul(r_ps[:, c * P:(c + 1) * P], rstd[:, c:c + 1].broadcast_to([P, P]), ident[:, :],
                                                start=True, stop=True)
                    last.then_inc(s["rb_ps"], 1)
                    if more:
                        h(ep, j + 1, range(1, MC))
                    if not (isinstance(ep, int) and ep * 4 + j == 0):
                        y(ep, j - 1)

                def y(ep, j):
                    slot, hs = j // 2 % 2, j % 2
                    if hs == 0:
                        pe.wait_ge(w2_e_s[slot], (tau * (E // 2) + ep + j // 4 + 1) * 16)
                    pe.wait_ge(s["a_done"], AHEAD + (tau * UNITS + ep * 4 + j + 1) * MC)
                    pe.wait_ge(s["y_free"], tau * Y + 2 + ep * 4 + j)
                    for c in range(SUB):
                        for m in range(MC):
                            last = nc.tensor.matmul(y_ps[:, c, :], hid[:, hs, m, c * P:(c + 1) * P], w2_sb[:, slot, m, :],
                                                    start=m == 0, stop=m == MC - 1)
                    last.then_inc(s["y_full"], 1)

                pipelined(lambda: h(0, 0, range(MC)), turn, lambda: y(E // 2 - 1, 3))(pe)

            def final(tau, par):
                for half in range(2):
                    i = m_fin(tau) + half * (3 + HB)
                    rows_ = slice(half * HB, (half + 1) * HB)
                    pe.wait_ge(s["m_free"], i)
                    for k in range(KC):
                        last = split3(m_ps[:, :].rearrange("p (b t) -> p b t", b=HB), wgd_hi[:, k, :], wgd_lo[:, k, :],
                                      xT_hi[:, par, k, rows_, HALO:], xT_lo[:, par, k, rows_, HALO:], k, KC)
                    last.then_inc(s["m_full"], 1)
                    for g in range(KC):
                        pe.wait_ge(s["m_free"], i + 1 + g)
                        nc.tensor.matmul(m_ps[:, :], wgu_sb[:, g * P:(g + 1) * P], gd_sb,
                                         start=True, stop=True).then_inc(s["m_full"], 1)
                    pe.wait_ge(s["og_done"], tau * 2 + half + 1)
                    for b in range(HB):
                        pe.wait_ge(s["m_free"], i + 3 + b)
                        for g in range(KC):
                            last = nc.tensor.matmul(m_ps[:, 0:D], gate_o[:, g, b * P:(b + 1) * P], wo_sb[:, g, :],
                                                    start=g == 0, stop=g == KC - 1)
                        last.then_inc(s["m_full"], 1)

            schedule(pe, prep, experts, final)

        @block.scalar
        def _(act):
            A = nc.scalar.activation
            act.wait_ge(s["setup_done"], 1)
            act.wait_ge(s["b1_ready"], 1)
            act.wait_ge(s["w1_out"], 16 * (E + 1))

            def gate_exp(tau):
                act.wait_ge(s["gmax"], tau + 1)
                A(expd[:, :, :].rearrange("p b e -> p (b e)"), shifted[:, :, :].rearrange("p b e -> p (b e)"),
                  ACT.Exp).then_inc(s["gexp"], 1)

            def prep(tau, par):
                def stats(b):
                    slot, n = b % XS, tau * B + b
                    act.wait_ge(x_in_s[slot], (tau * (B // XS) + b // XS + 1) * 16)
                    act.wait_ge(s["xstat"], n)
                    A(junk[:, :], x_in[:, slot, :], ACT.Identity, accum_out=stat[:, slot, 0:1]).then_inc(s["xsum"], 1)
                    act.wait_ge(s["xsum"], n + 1)
                    A(stat[:, slot, 1:2], stat[:, slot, 0:1], ACT.Copy, scale=-1.0 / D).then_inc(s["xneg"], 1)
                    act.wait_ge(s["xneg"], n + 1)
                    A(x_in[:, slot, :], x_in[:, slot, :], ACT.Identity, bias=stat[:, slot, 1:2]).then_inc(s["xctr"], 1)
                    act.wait_ge(s["xctr"], n + 1)
                    A(junk[:, :], x_in[:, slot, :], ACT.Square, accum_out=stat[:, slot, 2:3]).then_inc(s["xsq"], 1)
                    act.wait_ge(s["xsq"], n + 1)
                    A(stat[:, slot, 3:4], stat[:, slot, 2:3], ACT.Copy, scale=1.0 / D, bias=LN_EPS).then_inc(s["xstat"], 1)

                def norm(b):
                    act.wait_ge(s["xpow"], tau * B + b + 1)
                    A(acc[:, par, b, :], x_in[:, b % XS, :], ACT.Copy, scale=stat[:, b % XS, 4:5]).then_inc(s["xn_ready"], 1)

                slots_ = (m_ps, r_ps)
                for b in range(2):
                    stats(b)
                for b in range(2):
                    norm(b)
                for bp in range(B // 2):
                    coming = range(bp * 2 + 2, min(bp * 2 + 4, B))
                    for b in coming:
                        stats(b)
                    i = m_prep(tau) + bp * 4
                    for slot in range(2):
                        act.wait_ge(s["m_full"], i + slot + 1)
                        if bp > 0:
                            act.wait_ge(s["x_lo"], tau * B + bp * 2 + slot - 1)
                        A(xT32[:, slot, :, :].rearrange("p k t -> p (k t)"), slots_[slot][:, 0:D], ACT.Copy)
                        A(xT_hi[:, par, :, bp * 2 + slot, HALO:],
                          slots_[slot][:, 0:D].rearrange("p (k t) -> p k t", k=KC), ACT.Copy).then_inc(s["m_free"], 1)
                    for b in coming:
                        norm(b)
                    for slot in range(2):
                        act.wait_ge(s["m_full"], i + slot + 3)
                        A(logits[:, bp * 2 + slot, :], slots_[slot][:, 0:E], ACT.Copy).then_inc(s["m_free"], 1)
                act.wait_ge(s["y_added"], tau * Y)
                for g in range(GRP):
                    for half in range(2):
                        act.wait_ge(s["m_full"], m_prep(tau) + 2 * B + g * 2 + half + 1)
                        if not (isinstance(tau, int) and tau == 0 and g == 0):
                            act.wait_ge(qkv_out_s[half], (tau * GRP + g) * 16)
                        A(stage[:, half, :], slots_[half][:, :], ACT.Silu, bias=conv_b[:, g:g + 1]).then_inc(s["m_free"], 1)
                for half in range(2):
                    act.wait_ge(s["m_full"], m_prep(tau) + 2 * B + 2 * GRP + half + 1)
                    act.wait_ge(s["ab_out"], tau * 64)
                    A(ab_stage[:, half, :], slots_[half][0:2 * H, :], ACT.Sigmoid, bias=ab_b).then_inc(s["m_free"], 1)

            def experts(tau, par):
                for half in range(2):
                    act.wait_ge(qkv_out_s[half], (tau + 1) * GRP * 16)
                act.wait_ge(s["ab_out"], (tau + 1) * 64)
                if isinstance(tau, int) and tau == 0:
                    gate_exp(tau)
                for q in range(2):
                    i = m_exp(tau) + q
                    act.wait_ge(s["m_full"], i + 1)
                    A(combT[:, q, :], m_ps[:, 0:P], ACT.Copy).then_inc(s["m_free"], 1)
                    act.wait_ge(s["y_full"], FIRST + tau * Y + q + 1)
                    act.wait_ge(s["y_added"], tau * Y + q)
                    A(y_sb[:, :, :].rearrange("p c d -> p (c d)"), y_ps[:, :, :].rearrange("p c d -> p (c d)"),
                      ACT.Copy).then_inc(s["y_free"], 1)

                def evac(ep, j, m):
                    u = tau * UNITS + ep * 4 + j
                    act.wait_ge(s["h_done"], AHEAD + u * MC + m + 1)
                    b1_m = ecol_sb[:, j // 2 % 2, 2, m:m + 1]
                    A(hid[:, RAW, m, :], h_ps[:, m, :], ACT.Identity, bias=b1_m)
                    A(sq[:, m, :], h_ps[:, m, :], ACT.Square, bias=b1_m).then_inc(s["sq_done"], 1)

                def turn(ep, j):
                    u = tau * UNITS + ep * 4 + j
                    slot = j // 2 % 2
                    act.wait_ge(s["v_ps"], u + 1)
                    A(var_sb[:, :], r_ps[:, 0:SUB], ACT.Copy, bias=LN_EPS).then_inc(s["v_sb"], 1)
                    act.wait_ge(s["rb_ps"], u + 1)
                    A(rstd_b[:, :], r_ps[:, :], ACT.Copy).then_inc(s["rb_sb"], 1)
                    A(share[:, j % 4, :], comb[:, par, (j % 2) * HB:(j % 2 + 1) * HB, bass.ds(ep * 2 + j // 2, 1)].rearrange(
                        "p b o -> p (b o)"), ACT.Copy)
                    for m in range(MC):
                        act.wait_ge(s["t_done"], u * MC + m + 1)
                        if not (isinstance(ep, int) and ep * 4 + j == UNITS - 1):
                            evac(ep, j + 1, m)
                        A(hid[:, j % 2, m, :], hid[:, j % 2, m, :], ACT.Gelu, bias=ecol_sb[:, slot, 1, m:m + 1],
                          scale=ecol_sb[:, slot, 0, m:m + 1]).then_inc(s["a_done"], 1)
                    if not (isinstance(ep, int) and ep * 4 + j == 0):
                        y(ep, j - 1)

                def y(ep, j):
                    n = tau * Y + 2 + ep * 4 + j
                    act.wait_ge(s["y_full"], FIRST + n + 1)
                    act.wait_ge(s["y_added"], n)
                    for c in range(SUB):
                        last = A(y_sb[:, c, :], y_ps[:, c, :], ACT.Copy, scale=share[:, j % 4, c:c + 1])
                    last.then_inc(s["y_free"], 1)

                def first():
                    for m in range(MC):
                        evac(0, 0, m)

                pipelined(first, turn, lambda: y(E // 2 - 1, 3))(act)

            def final(tau, par):
                act.wait_ge(s["y_added"], (tau + 1) * Y)

                def stats(b):
                    n, slot = tau * B + b, b % 2
                    st = fstat[:, slot, :]
                    act.wait_ge(s["z_silu"], HAND + n - 1)
                    act.wait_ge(s["fsq"], FIRST + n)
                    A(junk[:, :], acc[:, par, b, :], ACT.Identity, accum_out=st[:, 0:1]).then_inc(s["fsum"], 1)
                    act.wait_ge(s["fsum"], n + 1)
                    A(st[:, 1:2], st[:, 0:1], ACT.Copy, scale=-1.0 / D).then_inc(s["fneg"], 1)
                    act.wait_ge(s["fneg"], n + 1)
                    A(z[:, slot, :], acc[:, par, b, :], ACT.Identity, bias=st[:, 1:2]).then_inc(s["fctr"], 1)
                    act.wait_ge(s["fctr"], n + 1)
                    A(junk[:, :], z[:, slot, :], ACT.Square, accum_out=st[:, 2:3]).then_inc(s["fsum2"], 1)
                    act.wait_ge(s["fsum2"], n + 1)
                    A(st[:, 3:4], st[:, 2:3], ACT.Copy, scale=1.0 / D, bias=LN_EPS).then_inc(s["fsq"], 1)

                for half in range(2):
                    i = m_fin(tau) + half * (3 + HB)
                    act.wait_ge(s["m_full"], i + 1)
                    A(gd_sb, m_ps[:, :], ACT.Silu).then_inc(s["m_free"], 1)
                    for g in range(KC):
                        act.wait_ge(s["m_full"], i + 2 + g)
                        A(gate_o[:, g, :], m_ps[:, :], ACT.Sigmoid).then_inc(s["m_free"], 1)
                    stats(half * HB)
                    for c in range(HB):
                        b = half * HB + c
                        n = tau * B + b
                        act.wait_ge(s["frstd"], n + 1)
                        A(z[:, c % 2, :], z[:, c % 2, :], ACT.Copy, scale=fstat[:, c % 2, 4:5]).then_inc(s["z_norm"], 1)
                        if c + 1 < HB:
                            stats(b + 1)
                        act.wait_ge(s["m_full"], i + 4 + c)
                        act.wait_ge(s["res_done"], n - 1 + HAND)
                        A(s_sb[:, c % 2, :], m_ps[:, 0:D], ACT.Copy).then_inc(s["m_free"], 1)
                        act.wait_ge(s["z_ready"], n + 1)
                        A(z2[:, c % 2, :], z[:, c % 2, :], ACT.Silu).then_inc(s["z_silu"], 1)
                        if b == B // 2 + 1 and not (isinstance(tau, int) and tau == NB - 1):
                            gate_exp(tau + 1)

            schedule(act, prep, experts, final)

        @block.gpsimd
        def _(pool):
            G = nc.gpsimd
            G.memset(ident[:, :], 0.0).then_inc(s["const_ready"], 1)
            G.memset(over_hid[:, :], 1.0 / HID).then_inc(s["const_ready"], 1)
            G.memset(below[:, :, :], 1.0).then_inc(s["const_ready"], 1)
            G.memset(minus_half[:, :], -0.5).then_inc(s["const_ready"], 1)
            G.memset(comb[:, :, :, :], 0.0).then_inc(s["const_ready"], 1)
            G.memset(combT[:, :, :], 0.0).then_inc(s["const_ready"], 1)
            pool.wait_ge(s["const_ready"], 3)
            G.affine_select(out=ident[:, :], in_=ident[:, :], compare_op=ALU.not_equal, fill=1.0, base=0,
                            pattern=[[-1, P]], channel_multiplier=1).then_inc(s["const_ready"], 1)
            G.affine_select(out=below[:, :, :], in_=below[:, :, :], compare_op=ALU.is_gt, fill=0.0, base=0,
                            pattern=[[1, E], [-1, E]], channel_multiplier=0).then_inc(s["const_ready"], 1)
            pool.wait_ge(s["w_in"], N_IN * 16)
            n = 0

            def split(hi, lo, full):
                nonlocal n
                G.tensor_copy(hi, full).then_inc(s["wsplit"], 1)
                pool.wait_ge(s["wsplit"], n + 1)
                G.tensor_tensor(lo, full, hi, ALU.subtract).then_inc(s["wsplit"], 1)
                n += 2

            for k in range(KC):
                for tap in range(TAPS):
                    pool.wait_ge(s["wsplit"], n)
                    G.tensor_tensor(wtap, wqkv_raw[:, k, :], taps_b[:, tap, :], ALU.mult).then_inc(s["wsplit"], 1)
                    n += 1
                    pool.wait_ge(s["wsplit"], n)
                    split(wp_hi[:, k, tap, :], wp_lo[:, k, tap, :], wtap)
            split(wab_hi[:, :, :], wab_lo[:, :, :], wab_raw)
            split(wgd_hi[:, :, :], wgd_lo[:, :, :], wgd_raw)
            for g in range(KC):
                G.tensor_scalar(wo_sb[:, g, :], wo_sb[:, g, :], rms_col[:, g:g + 1], None, ALU.mult).then_inc(s["wsplit"], 1)
                n += 1
            G.memset(xT_hi[:, 1, :, :, TB:], 0.0).then_inc(s["wsplit"], 1)
            G.memset(xT_lo[:, 1, :, :, TB:], 0.0).then_inc(s["wsplit"], 1)
            n += 2
            pool.wait_ge(s["wsplit"], n)
            G.memset(o_n[:, 0:1], 0.0).then_inc(s["setup_done"], 1)

            def prep(tau, par):
                for n_, part in enumerate((xT_hi, xT_lo)):
                    G.tensor_copy(part[:, par, :, :, 0:HALO], part[:, 1 - par, :, :, TB:]).then_inc(s["halo_done"], 1)
                def rstd_of(b):
                    slot, n = b % XS, tau * B + b
                    pool.wait_ge(s["xstat"], n + 1)
                    G.tensor_tensor(stat[:, slot, 4:5], stat[:, slot, 3:4], minus_half[:, 0:1], ALU.pow).then_inc(s["xpow"], 1)

                for b in range(2):
                    rstd_of(b)
                for bp in range(B // 2):
                    for b in range(bp * 2 + 2, min(bp * 2 + 4, B)):
                        rstd_of(b)
                    for slot in range(2):
                        b = bp * 2 + slot
                        pool.wait_ge(s["m_free"], m_prep(tau) + bp * 4 + slot + 1)
                        G.tensor_tensor(xT_lo[:, par, :, b, HALO:], xT32[:, slot, :, :],
                                        xT_hi[:, par, :, b, HALO:], ALU.subtract).then_inc(s["x_lo"], 1)

            def experts(tau, par):
                def add(n, half):
                    pool.wait_ge(s["y_free"], n + 1)
                    pool.wait_ge(s["y_added"], n)
                    a_ = acc[:, par, half * HB:(half + 1) * HB, :]
                    G.tensor_tensor(a_, a_, y_sb[:, :, :], ALU.add).then_inc(s["y_added"], 1)

                add(tau * Y, 0)

                def sums(ep, j):
                    u = tau * UNITS + ep * 4 + j
                    for q in range(2):
                        pool.wait_ge(s["sq_done"], u * MC + 2 * q + 2)
                        G.tensor_tensor(sq[:, 2 * q, :], sq[:, 2 * q, :], sq[:, 2 * q + 1, :], ALU.add).then_inc(s["sq_part"], 1)
                    pool.wait_ge(s["sq_part"], u * 2 + 2)
                    G.tensor_tensor(sq[:, 0, :], sq[:, 0, :], sq[:, 2, :], ALU.add).then_inc(s["sq_sum"], 1)

                def turn(ep, j):
                    u = tau * UNITS + ep * 4 + j
                    pool.wait_ge(s["v_sb"], u + 1)
                    G.tensor_tensor(rstd[:, :], var_sb[:, :], minus_half[:, 0:SUB], ALU.pow).then_inc(s["v_rstd"], 1)
                    pool.wait_ge(s["rb_sb"], FIRST + u + 1)
                    for m in range(MC):
                        G.tensor_tensor(hid[:, j % 2, m, :], hid[:, RAW, m, :], rstd_b[:, :], ALU.mult).then_inc(s["t_done"], 1)
                    if not (isinstance(ep, int) and ep * 4 + j == 0):
                        y(ep, j - 2)
                    if not (isinstance(ep, int) and ep * 4 + j == UNITS - 1):
                        sums(ep, j + 1)

                def y(ep, j):
                    add(tau * Y + 2 + ep * 4 + j, j % 2)

                def last():
                    y(E // 2 - 1, 2)
                    y(E // 2 - 1, 3)

                pipelined(lambda: sums(0, 0), turn, last)(pool)

            def final(tau, par):
                pool.wait_ge(s["oT_in"], (tau + 1) * 32)

                def rstd_of(b):
                    pool.wait_ge(s["fsq"], FIRST + tau * B + b + 1)
                    G.tensor_tensor(fstat[:, b % 2, 4:5], fstat[:, b % 2, 3:4], minus_half[:, 0:1], ALU.pow).then_inc(s["frstd"], 1)

                for half in range(2):
                    i = m_fin(tau) + half * (3 + HB)
                    for g in range(KC):
                        pool.wait_ge(s["m_free"], i + 2 + g)
                        last = G.tensor_tensor(gate_o[:, g, :].rearrange("p (b t) -> p b t", b=HB),
                                               gate_o[:, g, :].rearrange("p (b t) -> p b t", b=HB),
                                               oT_v[:, g, half * HB:(half + 1) * HB, :], ALU.mult)
                    last.then_inc(s["og_done"], 1)
                    rstd_of(half * HB)
                    for c in range(HB):
                        b = half * HB + c
                        n = tau * B + b
                        zc, z2c = z[:, c % 2, :], z2[:, c % 2, :]
                        pool.wait_ge(s["z_norm"], n + 1)
                        G.tensor_tensor(zc, zc, rows_sb[:, 0, :], ALU.mult).then_inc(s["fstep"], 1)
                        pool.wait_ge(s["fstep"], n * 2 + 1)
                        G.tensor_tensor(zc, zc, rows_sb[:, 1, :], ALU.add).then_inc(s["z_ready"], 1)
                        if c + 1 < HB:
                            rstd_of(b + 1)
                        pool.wait_ge(s["z_silu"], HAND + n + 1)
                        pool.wait_ge(s["m_free"], i + 4 + c)
                        pool.wait_ge(x_res_s[c % 2], (tau * (B // 2) + b // 2 + 1) * 16)
                        pool.wait_ge(out_s[c % 2], (FIRST + tau * (B // 2) + b // 2) * 16)
                        G.tensor_tensor(z2c, z2c, s_sb[:, c % 2, :], ALU.mult).then_inc(s["fstep"], 1)
                        pool.wait_ge(s["fstep"], n * 2 + 2)
                        G.tensor_tensor(res[:, c % 2, :], z2c, x_res[:, c % 2, :], ALU.add).then_inc(s["res_done"], 1)

            schedule(pool, prep, experts, final)

        @block.vector
        def _(dve):
            V = nc.vector
            d = [0]

            def setup(ins):
                ins.then_inc(s["dsetup"], 1)
                d[0] += 1
                dve.wait_ge(s["dsetup"], d[0])

            dve.wait_ge(s["w_in"], N_IN * 16)
            dve.wait_ge(s["b1_ps"], 1)
            setup(V.tensor_reduce(b1_mean[:, :], r_ps[:, 0:E * MC].rearrange("p (e m) -> p e m", m=MC), AX, ALU.add))
            V.tensor_tensor(b1_col, b1_col,
                            b1_mean[:, :].rearrange("p (e o) -> p e o", o=1).broadcast_to([P, E, MC]),
                            ALU.subtract).then_inc(s["b1_ready"], 1)
            for e in range(E):
                for k in range(KC):
                    c = e * KC + k
                    dve.wait_ge(w1_raw_s[k], (e + 1) * 16)
                    setup(V.tensor_reduce(w_mean[:, c:c + 1], w1_raw[:, k, :], AX, ALU.add))
                    setup(V.tensor_scalar(w_mean[:, c:c + 1], w_mean[:, c:c + 1], 1.0 / HID, None, ALU.mult))
                    V.tensor_scalar(w1_ctr, w1_raw[:, k, :], w_mean[:, c:c + 1], None, ALU.subtract).then_inc(s["w1_free"], 1)
                    dve.wait_ge(s["w1_free"], c + 1)
                    if e:
                        dve.wait_ge(s["w1_out"], e * 16)
                    setup(V.tensor_copy(w1_parts[:, 0, k, :], w1_ctr))
                    if k == KC - 1:
                        V.tensor_tensor(w1_parts[:, 1, k, :], w1_ctr, w1_parts[:, 0, k, :], ALU.subtract).then_inc(s["w1_split"], 1)
                        dve.wait_ge(s["w1_split"], e + 1)
                    else:
                        setup(V.tensor_tensor(w1_parts[:, 1, k, :], w1_ctr, w1_parts[:, 0, k, :], ALU.subtract))
            setup(V.memset(state[:, 0, :, :], 0.0))
            dve.wait_ge(s["setup_done"], 1)
            dve.wait_ge(s["const_ready"], N_CONST)

            def heads(tau, par):
                hs = tau * HEAD_STEPS
                k_, q_, v_ = kq[:, par, 0, :, :], kq[:, par, 1, :, :], bv[:, par, :, :]
                n = [0]

                def go(ins):
                    ins.then_inc(s["head_step"], 1)
                    n[0] += 1
                    dve.wait_ge(s["head_step"], hs + n[0])

                def dot(out_, a_, b_):
                    go(V.tensor_tensor(head_tmp[:, :, :], a_, b_, ALU.mult))
                    go(V.tensor_reduce(out_, head_tmp[:, :, :].rearrange("p d t -> p t d"), AX, ALU.add))

                dve.wait_ge(s["heads_in"], (tau + 1) * 5 * 16)
                dot(head_norm[:, 0, :], k_, k_)
                dot(head_norm[:, 1, :], q_, q_)
                dot(c_qk[:, par, :], k_, q_)
                go(V.tensor_scalar(head_norm[:, :, :], head_norm[:, :, :], NORM_MIN, None, ALU.max))
                go(V.tensor_scalar(r_kq[:, :, :].bitcast(I32), head_norm[:, :, :].bitcast(I32), -0.5, MAGIC, ALU.mult, ALU.add))
                for _ in range(3):
                    go(V.scalar_tensor_tensor(out=head_sq[:, :, :], in0=r_kq[:, :, :], scalar=-0.5, in1=r_kq[:, :, :],
                                              op0=ALU.mult, op1=ALU.mult))
                    go(V.tensor_tensor(head_sq[:, :, :], head_sq[:, :, :], head_norm[:, :, :], ALU.mult))
                    go(V.scalar_tensor_tensor(out=r_kq[:, :, :], in0=head_sq[:, :, :], scalar=1.5, in1=r_kq[:, :, :],
                                              op0=ALU.add, op1=ALU.mult))
                go(V.tensor_scalar(decay[:, par, :], decay[:, par, :], 0.1, 1.0, ALU.max, ALU.min))
                go(V.scalar_tensor_tensor(out=beta[:, :], in0=beta[:, :], scalar=1.0, in1=r_kq[:, 0, :], op0=ALU.min, op1=ALU.mult))
                go(V.scalar_tensor_tensor(out=c_v[:, par, :], in0=beta[:, :], scalar=-1.0, in1=r_kq[:, 0, :], op0=ALU.mult, op1=ALU.mult))
                go(V.tensor_tensor(v_, v_, beta[:, :].rearrange("p (o t) -> p o t", o=1).broadcast_to([P, DH, TB]), ALU.mult))
                go(V.tensor_tensor(c_q[:, par, :], decay[:, par, :], r_kq[:, 1, :], ALU.mult))
                go(V.tensor_tensor(c_qk[:, par, :], c_qk[:, par, :], r_kq[:, 1, :], ALU.mult))
                assert n[0] == HEAD_STEPS, n[0]

            def gating(tau, par):
                gs = tau * GATE_STEPS
                n = [0]

                def go(ins):
                    ins.then_inc(s["dgate"], 1)
                    n[0] += 1
                    dve.wait_ge(s["dgate"], gs + n[0])

                def bc(ap, shape, where):
                    return ap.rearrange(where, o=1).broadcast_to(shape)

                full = [P, B, E, E]
                go(V.tensor_reduce(lmax[:, :], logits[:, :, :], AX, ALU.max))
                V.tensor_tensor(shifted[:, :, :], logits[:, :, :], bc(lmax[:, :], [P, B, E], "p (b o) -> p b o"),
                                ALU.subtract).then_inc(s["gmax"], 1)
                dve.wait_ge(s["gmax"], tau + 1)
                other = shifted[:, :, :].rearrange("p b (o f) -> p b o f", o=1).broadcast_to(full)
                own = shifted[:, :, :].rearrange("p b (e o) -> p b e o", o=1).broadcast_to(full)
                go(V.tensor_tensor(cmp_gt[:, :, :, :], other, own, ALU.is_gt))
                go(V.tensor_tensor(cmp_eq[:, :, :, :], other, own, ALU.is_equal))
                go(V.tensor_tensor(cmp_eq[:, :, :, :], cmp_eq[:, :, :, :],
                                   below[:, :, :].rearrange("p (o e) f -> p o e f", o=1).broadcast_to(full), ALU.mult))
                go(V.tensor_tensor(cmp_gt[:, :, :, :], cmp_gt[:, :, :, :], cmp_eq[:, :, :, :], ALU.add))
                go(V.tensor_reduce(rank[:, :, :], cmp_gt[:, :, :, :], AX, ALU.add))
                go(V.tensor_scalar(rank[:, :, :], rank[:, :, :], 1.5, None, ALU.is_lt))
                dve.wait_ge(s["gexp"], tau + 1)
                go(V.tensor_tensor(rank[:, :, :], rank[:, :, :], expd[:, :, :], ALU.mult))
                go(V.tensor_reduce(csum[:, :], rank[:, :, :], AX, ALU.add))
                go(V.reciprocal(csum[:, :], csum[:, :]))
                V.tensor_tensor(comb[:, par, :, 0:E], rank[:, :, :], bc(csum[:, :], [P, B, E], "p (b o) -> p b o"),
                                ALU.mult).then_inc(s["comb_ready"], 1)
                assert n[0] == GATE_STEPS, n[0]

            def recurrence(tau, par):
                heads(tau, par)
                gating(tau, par)
                k_all, q_all = kq[:, par, 0, :, :], kq[:, par, 1, :, :]
                with dve.Fori(0, NG) as grp:
                    base = (tau * NG + grp) * GROUP_STEPS
                    n = [0]

                    def do(ins):
                        ins.then_inc(s["step"], 1)
                        n[0] += 1
                        return n[0]

                    def done(k_):
                        dve.wait_ge(s["step"], FIRST + OUT_STEPS + base + k_)

                    for i in range(GT):
                        t = bass.ds(grp * GT + i, 1)
                        S_in, S_out = state[:, i % 2, :, :], state[:, (i + 1) % 2, :, :]
                        k_t = k_all[:, :, t].rearrange("p i o -> p o i").broadcast_to([P, DH, DH])
                        q_t = q_all[:, :, t].rearrange("p i o -> p o i")
                        hw = DH // 2
                        done(n[0] if i else -OUT_STEPS)
                        a1 = do(V.tensor_tensor(prod_k[:, :, :], S_in, k_t, ALU.mult))
                        do(V.tensor_tensor(prod_q[:, 0:hw, :], S_in[:, 0:hw, :], q_t.broadcast_to([P, hw, DH]), ALU.mult))
                        done(a1)
                        a3 = do(V.tensor_reduce(ks[:, :], prod_k[:, :, :], AX, ALU.add))
                        a4 = do(V.tensor_tensor(prod_q[:, hw:, :], S_in[:, hw:, :], q_t.broadcast_to([P, hw, DH]), ALU.mult))
                        done(a3)
                        a5 = do(V.scalar_tensor_tensor(out=upd[:, i, :], in0=ks[:, :], scalar=c_v[:, par, t],
                                                       in1=bv[:, par, :, t].rearrange("p j o -> p (j o)"),
                                                       op0=ALU.mult, op1=ALU.add))
                        do(V.tensor_reduce(qs[:, i, 0:hw], prod_q[:, 0:hw, :], AX, ALU.add))
                        done(a5)
                        a7 = do(V.tensor_tensor(outer[:, :, :],
                                                upd[:, i, :].rearrange("p (j o) -> p j o", o=1).broadcast_to([P, DH, DH]),
                                                k_t, ALU.mult))
                        a8 = do(V.tensor_reduce(qs[:, i, hw:], prod_q[:, hw:, :], AX, ALU.add))
                        done(a7)
                        do(V.scalar_tensor_tensor(out=S_out, in0=S_in, scalar=decay[:, par, t], in1=outer[:, :, :],
                                                  op0=ALU.mult, op1=ALU.add))
                    ts_ = bass.ds(grp * GT, GT)

                    def per_token(ap):
                        return ap[:, par, ts_].rearrange("p (t o) -> p t o", o=1).broadcast_to([P, GT, DH])

                    o_view = q_all[:, :, ts_].rearrange("p j t -> p t j")
                    done(a8)
                    b1 = do(V.tensor_tensor(o_t1[:, :, :], qs[:, :, :], per_token(c_q), ALU.mult))
                    b2_ = do(V.tensor_tensor(o_t2[:, :, :], upd[:, :, :], per_token(c_qk), ALU.mult))
                    done(b2_)
                    do(V.tensor_tensor(o_view, o_t1[:, :, :], o_t2[:, :, :], ALU.add))
                    assert n[0] == GROUP_STEPS, n[0]
                bs = tau * BLOCK_STEPS
                n = [0]

                def go(ins):
                    ins.then_inc(s["block_step"], 1)
                    n[0] += 1
                    dve.wait_ge(s["block_step"], bs + n[0])

                dve.wait_ge(s["step"], FIRST + OUT_STEPS + (tau + 1) * (NG * GROUP_STEPS))
                go(V.tensor_tensor(head_tmp[:, :, :], q_all, q_all, ALU.mult))
                go(V.tensor_reduce(o_ms[:, :], head_tmp[:, :, :].rearrange("p d t -> p t d"), AX, ALU.add))
                go(V.tensor_scalar(o_ms[:, :], o_ms[:, :], 1.0 / DH, RMS_EPS, ALU.mult, ALU.add))
                go(V.tensor_scalar(o_r[:, :].bitcast(I32), o_ms[:, :].bitcast(I32), -0.5, MAGIC, ALU.mult, ALU.add))
                for _ in range(3):
                    go(V.scalar_tensor_tensor(out=o_n[:, :], in0=o_r[:, :], scalar=-0.5, in1=o_r[:, :], op0=ALU.mult, op1=ALU.mult))
                    go(V.tensor_tensor(o_n[:, :], o_n[:, :], o_ms[:, :], ALU.mult))
                    go(V.scalar_tensor_tensor(out=o_r[:, :], in0=o_n[:, :], scalar=1.5, in1=o_r[:, :], op0=ALU.add, op1=ALU.mult))
                V.tensor_tensor(q_all, q_all,
                                o_r[:, :].rearrange("p (o t) -> p o t", o=1).broadcast_to([P, DH, TB]),
                                ALU.mult).then_inc(s["o_ready"], 1)
                assert n[0] == BLOCK_STEPS, n[0]

            with dve.Fori(0, NB // 2) as m:
                for par in range(2):
                    recurrence_tau = m * 2 + par
                    recurrence(recurrence_tau, par)


def kernel(**inputs):
    import numpy as np
    import concourse.bacc as bacc
    from concourse.bass_utils import run_bass_kernel_spmd

    a = {k[3:]: np.asarray(v) for k, v in inputs.items()}
    f = {k[5:] if k.startswith("attn_") else k[4:] + "_f": v for k, v in a.items()}

    def by_partition(v, chunks):
        return v.reshape(chunks, P).T

    ab = np.zeros((P, 1), np.float32)
    ab[0:H, 0], ab[H:2 * H, 0] = f["ba"], f["bb"]
    cols = np.concatenate(
        [by_partition(f[n], KC) for n in ("qcb", "kcb", "vcb")] + [ab, by_partition(f["rms_w"].reshape(-1), KC)]
        + [by_partition(f[n][e], MC) for e in range(E) for n in ("ln1_g_f", "ln1_b_f", "b1_f")], axis=1)
    arrays = {
        "x": f["x"],
        "wqkv": np.concatenate([f["Wq"], f["Wk"], f["Wv"]], axis=1),
        "cw": np.concatenate([f["qcw"], f["kcw"], f["vcw"]], axis=0).T,
        "wab": np.concatenate([f["Wa"], f["Wb"]], axis=1),
        "wgd": f["Wgd"], "wgu": f["Wgu"], "wo": f["Wo"], "gate": f["gate_w_f"],
        "w1": f["w1_f"], "w2": f["w2_f"], "b2": f["b2_f"],
        "rows": np.stack([f["ln_g_f"], f["ln_b_f"]]),
        "cols": cols,
    }
    nc = bacc.Bacc("TRN2", target_bir_lowering=False, num_devices=1)
    maps, args = {}, []
    for name, v in arrays.items():
        v = np.ascontiguousarray(v)
        maps[f"in_{name}"] = v
        args.append(nc.dram_tensor(f"in_{name}", v.shape, mybir.dt.from_np(v.dtype), kind="ExternalInput").ap())
    out = nc.dram_tensor("out_0", f["x"].shape, F32, kind="ExternalOutput").ap()
    bass_delta_moe(nc, *args, out)
    r = run_bass_kernel_spmd(nc, [maps], core_ids=[0])
    return r.results[0]["out_0"]
```
